# Optimizing a Trainium2 kernel written in Bass

```python
import numpy as np
import jax
import jax.numpy as jnp

def _softmax(x, axis=-1):
    return jax.nn.softmax(x, axis=axis)

def _gelu(x):
    return jax.nn.gelu(x, approximate=True)

def _silu(x):
    return jax.nn.silu(x)

def _sigmoid(x):
    return jax.nn.sigmoid(x)

def _layernorm(x, axis=-1, eps=1e-05):
    m = jnp.mean(x, axis=axis, keepdims=True)
    v = jnp.var(x, axis=axis, keepdims=True)
    return (x - m) / jnp.sqrt(v + eps)

def _scatter_add(tgt, idx, src, axis=0):
    return tgt.at[idx].add(src)

def _segment_sum(src, seg, n):
    return jax.ops.segment_sum(src, seg, n)
kernel_name = 'mk_lm_tower_d1_tok_ids768_r4_4eda05'

def setup_inputs(seed: int=0):
    np.random.seed(seed)
    _w = jnp.asarray

    def _rec_inputs():
        import jax
        import jax.numpy as jnp
        _rk = jax.random.key(seed)
        x = jax.random.randint(jax.random.fold_in(_rk, 1), (32, 128), 0, 30522, jnp.int32)
        mask_BS_i1_0 = jnp.where(jnp.ones((32, 128), dtype=bool), 1, 0).astype(jnp.int32)
        return (x, mask_BS_i1_0)
    x, mask_BS_i1_0 = _rec_inputs()

    def _L0_tok_setup():
        import jax, jax.numpy as jnp
        import numpy as np
        VOCAB = 30522
        HIDDEN = 192
        MAX_POS = 128
        TYPE_VOCAB = 2
        EPS = 1e-05
        key = jax.random.key(seed)
        k1, k2, k3, k4, k5 = jax.random.split(key, 5)
        B, S = (32, 128)
        return {'input_ids': jax.random.randint(k1, (B, S), 0, VOCAB, dtype=jnp.int64 if jax.config.jax_enable_x64 else jnp.int32), 'token_type_ids': jax.random.randint(k2, (B, S), 0, TYPE_VOCAB, dtype=jnp.int32), 'tok_w': jax.random.normal(k3, (VOCAB, HIDDEN), dtype=jnp.float32), 'pos_w': jax.random.normal(k4, (MAX_POS, HIDDEN), dtype=jnp.float32), 'type_w': jax.random.normal(k5, (TYPE_VOCAB, HIDDEN), dtype=jnp.float32), 'gamma': jnp.ones((HIDDEN,), dtype=jnp.float32), 'beta': jnp.zeros((HIDDEN,), dtype=jnp.float32)}
    _L0_tok_all = _L0_tok_setup()
    _L0_tok_in = {k: v for k, v in _L0_tok_all.items() if k in ('tok_w', 'pos_w', 'type_w', 'gamma', 'beta')}
    del _L0_tok_all

    def _L0_attn_setup():
        import jax, jax.numpy as jnp
        import numpy as np
        from jax import lax
        H = 192
        I = 384
        N = 16
        R = 48
        K = 4
        NL = 16
        B, L = (2, 256)
        EPS = 1e-05

        def rmsnorm(x, w):
            return x * lax.rsqrt(jnp.mean(x * x, axis=-1, keepdims=True) + EPS) * w

        def causal_conv(u, w, b):
            uc = jnp.swapaxes(u, 1, 2)
            y = lax.conv_general_dilated(uc, w, (1,), [(K - 1, 0)], dimension_numbers=('NCH', 'OIH', 'NCH'), feature_group_count=I)
            return jnp.swapaxes(y + b[None, :, None], 1, 2)

        def selective_scan(u, dt, A, Bm, Cm, Dp):

            def step(h, inp):
                u_t, dt_t, B_t, C_t = inp
                dA = jnp.exp(dt_t[:, :, None] * A)
                h = dA * h + (dt_t * u_t)[:, :, None] * B_t[:, None, :]
                y = jnp.einsum('bin,bn->bi', h, C_t)
                return (h, y)
            inputs = tuple((jnp.moveaxis(a, 1, 0) for a in (u, dt, Bm, Cm)))
            h0 = jnp.zeros((u.shape[0],) + A.shape, u.dtype)
            _, ys = lax.scan(step, h0, inputs)
            return jnp.moveaxis(ys, 0, 1) + u * Dp

        def mamba_layer(x, p):
            in_w, cw, cb, xp_w, dtw, dtb, a_log, dp, ow, nw = p
            h = rmsnorm(x, nw)
            xz = jnp.einsum('blh,ch->blc', h, in_w)
            u, z = jnp.split(xz, 2, axis=-1)
            u = jax.nn.silu(causal_conv(u, cw, cb))
            proj = jnp.einsum('bli,ci->blc', u, xp_w)
            dt_r, Bm, Cm = (proj[..., :R], proj[..., R:R + N], proj[..., R + N:])
            dt = jax.nn.softplus(jnp.einsum('blr,ir->bli', dt_r, dtw) + dtb)
            A = -jnp.exp(a_log)
            y = selective_scan(u, dt, A, Bm, Cm, dp)
            y = y * jax.nn.silu(z)
            return x + jnp.einsum('bli,hi->blh', y, ow)
        key = jax.random.key(seed)
        ks = jax.random.split(key, 8)
        s = 0.02
        x = jax.random.normal(ks[0], (B, L, H), jnp.float32)
        in_proj_w = jax.random.normal(ks[1], (NL, 2 * I, H), jnp.float32) * s
        conv_w = jax.random.normal(ks[2], (NL, I, 1, K), jnp.float32) * 0.1
        conv_b = jnp.zeros((NL, I), jnp.float32)
        x_proj_w = jax.random.normal(ks[3], (NL, R + 2 * N, I), jnp.float32) * s
        dt_proj_w = jax.random.normal(ks[4], (NL, I, R), jnp.float32) * 0.01
        dt_proj_b = -4.0 + 0.1 * jax.random.normal(ks[5], (NL, I), jnp.float32)
        A_log = jnp.log(jnp.tile(jnp.arange(1, N + 1, dtype=jnp.float32), (NL, I, 1)))
        D = jnp.ones((NL, I), jnp.float32)
        out_proj_w = jax.random.normal(ks[6], (NL, H, I), jnp.float32) * s
        norm_w = jnp.ones((NL, H), jnp.float32)
        final_norm_w = jnp.ones((H,), jnp.float32)
        return {'x': x, 'in_proj_w': in_proj_w, 'conv_w': conv_w, 'conv_b': conv_b, 'x_proj_w': x_proj_w, 'dt_proj_w': dt_proj_w, 'dt_proj_b': dt_proj_b, 'A_log': A_log, 'D': D, 'out_proj_w': out_proj_w, 'norm_w': norm_w, 'final_norm_w': final_norm_w}
    _L0_attn_all = _L0_attn_setup()
    _L0_attn_in = {k: v for k, v in _L0_attn_all.items() if k in ('in_proj_w', 'conv_w', 'conv_b', 'x_proj_w', 'dt_proj_w', 'dt_proj_b', 'A_log', 'D', 'out_proj_w', 'norm_w', 'final_norm_w')}
    del _L0_attn_all

    def _L0_ffn_setup():
        import jax, jax.numpy as jnp
        import numpy as np
        B, T, D = (2, 512, 192)
        S, R, M, K = (8, 16, 64, 4)
        H, G = (32, 64)

        def _ssinf3(x, P, C, W1, b1, W2, b2, G1, g1b, G2, g2b):
            shp = x.shape
            xf = x.reshape(-1, shp[-1])
            z = jnp.einsum('nd,sdr->nsr', xf, P)
            scores = jnp.einsum('nsr,smr->nsm', z, C)
            topv, topi = jax.lax.top_k(scores, K)
            w = jax.nn.softmax(topv, axis=-1)
            sidx = jnp.arange(S)[None, :, None]
            W1g = W1[sidx, topi]
            b1g = b1[sidx, topi]
            W2g = W2[sidx, topi]
            b2g = b2[sidx, topi]
            h = jax.nn.gelu(jnp.einsum('nsr,nskrh->nskh', z, W1g) + b1g)
            yl = jnp.einsum('nskh,nskhr->nskr', h, W2g) + b2g
            comb = jnp.einsum('nskr,nsk->nsr', yl, w)
            comb = comb.reshape(xf.shape[0], S * R)
            out = jax.nn.gelu(comb @ G1 + g1b) @ G2 + g2b
            return out.reshape(shp)
        key = jax.random.key(seed)
        k = jax.random.split(key, 8)
        rn = lambda kk, shape, s: jax.random.normal(kk, shape, dtype=jnp.float32) * s
        return {'x': rn(k[0], (B, T, D), 1.0), 'P': rn(k[1], (S, D, R), D ** (-0.5)), 'C': rn(k[2], (S, M, R), R ** (-0.5)), 'W1': rn(k[3], (S, M, R, H), R ** (-0.5)), 'b1': jnp.zeros((S, M, H), jnp.float32), 'W2': rn(k[4], (S, M, H, R), H ** (-0.5)), 'b2': jnp.zeros((S, M, R), jnp.float32), 'G1': rn(k[5], (S * R, G), (S * R) ** (-0.5)), 'g1b': jnp.zeros((G,), jnp.float32), 'G2': rn(k[6], (G, D), G ** (-0.5)), 'g2b': jnp.zeros((D,), jnp.float32)}
    _L0_ffn_all = _L0_ffn_setup()
    _L0_ffn_in = {k: v for k, v in _L0_ffn_all.items() if k in ('P', 'C', 'W1', 'b1', 'W2', 'b2', 'G1', 'g1b', 'G2', 'g2b')}
    del _L0_ffn_all
    return {'x': x, 'mask_BS_i1_0': mask_BS_i1_0, 'L0_tok_tok_w': _L0_tok_in['tok_w'], 'L0_tok_pos_w': _L0_tok_in['pos_w'], 'L0_tok_type_w': _L0_tok_in['type_w'], 'L0_tok_gamma': _L0_tok_in['gamma'], 'L0_tok_beta': _L0_tok_in['beta'], 'L0_attn_in_proj_w': _L0_attn_in['in_proj_w'], 'L0_attn_conv_w': _L0_attn_in['conv_w'], 'L0_attn_conv_b': _L0_attn_in['conv_b'], 'L0_attn_x_proj_w': _L0_attn_in['x_proj_w'], 'L0_attn_dt_proj_w': _L0_attn_in['dt_proj_w'], 'L0_attn_dt_proj_b': _L0_attn_in['dt_proj_b'], 'L0_attn_A_log': _L0_attn_in['A_log'], 'L0_attn_D': _L0_attn_in['D'], 'L0_attn_out_proj_w': _L0_attn_in['out_proj_w'], 'L0_attn_norm_w': _L0_attn_in['norm_w'], 'L0_attn_final_norm_w': _L0_attn_in['final_norm_w'], 'L0_ffn_P': _L0_ffn_in['P'], 'L0_ffn_C': _L0_ffn_in['C'], 'L0_ffn_W1': _L0_ffn_in['W1'], 'L0_ffn_b1': _L0_ffn_in['b1'], 'L0_ffn_W2': _L0_ffn_in['W2'], 'L0_ffn_b2': _L0_ffn_in['b2'], 'L0_ffn_G1': _L0_ffn_in['G1'], 'L0_ffn_g1b': _L0_ffn_in['g1b'], 'L0_ffn_G2': _L0_ffn_in['G2'], 'L0_ffn_g2b': _L0_ffn_in['g2b']}

def reference(x, mask_BS_i1_0, L0_tok_tok_w, L0_tok_pos_w, L0_tok_type_w, L0_tok_gamma, L0_tok_beta, L0_attn_in_proj_w, L0_attn_conv_w, L0_attn_conv_b, L0_attn_x_proj_w, L0_attn_dt_proj_w, L0_attn_dt_proj_b, L0_attn_A_log, L0_attn_D, L0_attn_out_proj_w, L0_attn_norm_w, L0_attn_final_norm_w, L0_ffn_P, L0_ffn_C, L0_ffn_W1, L0_ffn_b1, L0_ffn_W2, L0_ffn_b2, L0_ffn_G1, L0_ffn_g1b, L0_ffn_G2, L0_ffn_g2b):
    import jax
    import jax.numpy as jnp

    def _L0_tok_ref(input_ids, token_type_ids, tok_w, pos_w, type_w, gamma, beta):
        import jax, jax.numpy as jnp
        import numpy as np
        VOCAB = 30522
        HIDDEN = 192
        MAX_POS = 128
        TYPE_VOCAB = 2
        EPS = 1e-05
        S = input_ids.shape[-1]
        emb = tok_w[input_ids] + pos_w[jnp.arange(S)] + type_w[token_type_ids]
        mean = jnp.mean(emb, axis=-1, keepdims=True)
        var = jnp.mean(jnp.square(emb - mean), axis=-1, keepdims=True)
        out = (emb - mean) * gamma * jax.lax.rsqrt(var + EPS) + beta
        return out

    def _L0_attn_ref(x, in_proj_w, conv_w, conv_b, x_proj_w, dt_proj_w, dt_proj_b, A_log, D, out_proj_w, norm_w, final_norm_w):
        import jax, jax.numpy as jnp
        import numpy as np
        from jax import lax
        H = 192
        I = 384
        N = 16
        R = 48
        K = 4
        NL = 16
        B, L = (2, 256)
        EPS = 1e-05

        def rmsnorm(x, w):
            return x * lax.rsqrt(jnp.mean(x * x, axis=-1, keepdims=True) + EPS) * w

        def causal_conv(u, w, b):
            uc = jnp.swapaxes(u, 1, 2)
            y = lax.conv_general_dilated(uc, w, (1,), [(K - 1, 0)], dimension_numbers=('NCH', 'OIH', 'NCH'), feature_group_count=I)
            return jnp.swapaxes(y + b[None, :, None], 1, 2)

        def selective_scan(u, dt, A, Bm, Cm, Dp):

            def step(h, inp):
                u_t, dt_t, B_t, C_t = inp
                dA = jnp.exp(dt_t[:, :, None] * A)
                h = dA * h + (dt_t * u_t)[:, :, None] * B_t[:, None, :]
                y = jnp.einsum('bin,bn->bi', h, C_t)
                return (h, y)
            inputs = tuple((jnp.moveaxis(a, 1, 0) for a in (u, dt, Bm, Cm)))
            h0 = jnp.zeros((u.shape[0],) + A.shape, u.dtype)
            _, ys = lax.scan(step, h0, inputs)
            return jnp.moveaxis(ys, 0, 1) + u * Dp

        def mamba_layer(x, p):
            in_w, cw, cb, xp_w, dtw, dtb, a_log, dp, ow, nw = p
            h = rmsnorm(x, nw)
            xz = jnp.einsum('blh,ch->blc', h, in_w)
            u, z = jnp.split(xz, 2, axis=-1)
            u = jax.nn.silu(causal_conv(u, cw, cb))
            proj = jnp.einsum('bli,ci->blc', u, xp_w)
            dt_r, Bm, Cm = (proj[..., :R], proj[..., R:R + N], proj[..., R + N:])
            dt = jax.nn.softplus(jnp.einsum('blr,ir->bli', dt_r, dtw) + dtb)
            A = -jnp.exp(a_log)
            y = selective_scan(u, dt, A, Bm, Cm, dp)
            y = y * jax.nn.silu(z)
            return x + jnp.einsum('bli,hi->blh', y, ow)
        params = (in_proj_w, conv_w, conv_b, x_proj_w, dt_proj_w, dt_proj_b, A_log, D, out_proj_w, norm_w)

        def body(carry, p):
            return (mamba_layer(carry, p), None)
        out, _ = lax.scan(body, x, params)
        return rmsnorm(out, final_norm_w)

    def _L0_ffn_ref(x, P, C, W1, b1, W2, b2, G1, g1b, G2, g2b):
        import jax, jax.numpy as jnp
        import numpy as np
        B, T, D = (2, 512, 192)
        S, R, M, K = (8, 16, 64, 4)
        H, G = (32, 64)

        def _ssinf3(x, P, C, W1, b1, W2, b2, G1, g1b, G2, g2b):
            shp = x.shape
            xf = x.reshape(-1, shp[-1])
            z = jnp.einsum('nd,sdr->nsr', xf, P)
            scores = jnp.einsum('nsr,smr->nsm', z, C)
            topv, topi = jax.lax.top_k(scores, K)
            w = jax.nn.softmax(topv, axis=-1)
            sidx = jnp.arange(S)[None, :, None]
            W1g = W1[sidx, topi]
            b1g = b1[sidx, topi]
            W2g = W2[sidx, topi]
            b2g = b2[sidx, topi]
            h = jax.nn.gelu(jnp.einsum('nsr,nskrh->nskh', z, W1g) + b1g)
            yl = jnp.einsum('nskh,nskhr->nskr', h, W2g) + b2g
            comb = jnp.einsum('nskr,nsk->nsr', yl, w)
            comb = comb.reshape(xf.shape[0], S * R)
            out = jax.nn.gelu(comb @ G1 + g1b) @ G2 + g2b
            return out.reshape(shp)
        return _ssinf3(x, P, C, W1, b1, W2, b2, G1, g1b, G2, g2b)
    h = _L0_tok_ref(x, mask_BS_i1_0, L0_tok_tok_w, L0_tok_pos_w, L0_tok_type_w, L0_tok_gamma, L0_tok_beta)
    h = h + _L0_attn_ref(_layernorm(h, axis=-1), L0_attn_in_proj_w, L0_attn_conv_w, L0_attn_conv_b, L0_attn_x_proj_w, L0_attn_dt_proj_w, L0_attn_dt_proj_b, L0_attn_A_log, L0_attn_D, L0_attn_out_proj_w, L0_attn_norm_w, L0_attn_final_norm_w)
    h = h + _L0_ffn_ref(_layernorm(h, axis=-1), L0_ffn_P, L0_ffn_C, L0_ffn_W1, L0_ffn_b1, L0_ffn_W2, L0_ffn_b2, L0_ffn_G1, L0_ffn_g1b, L0_ffn_G2, L0_ffn_g2b)
    return h

_drawn_inputs = setup_inputs


def setup_inputs(seed=0):
    import zlib

    import numpy as np

    out = dict(_drawn_inputs(seed))
    spreads = {'L0_tok_gamma': (1.0, 0.2),
     'L0_tok_beta': (0.0, 0.1),
     'L0_attn_conv_b': (0.0, 0.8),
     'L0_attn_D': (1.0, 0.6),
     'L0_attn_norm_w': (1.0, 0.6),
     'L0_attn_final_norm_w': (1.0, 0.2),
     'L0_ffn_b1': (0.0, 0.8),
     'L0_ffn_b2': (0.0, 0.531),
     'L0_ffn_g1b': (0.0, 0.272),
     'L0_ffn_g2b': (0.0, 0.1)}
    factors = {'L0_attn_in_proj_w': 6.078,
     'L0_attn_conv_w': 8.0,
     'L0_attn_x_proj_w': 8.0,
     'L0_attn_dt_proj_w': 8.0,
     'L0_attn_dt_proj_b': 8.0,
     'L0_attn_A_log': 8.0,
     'L0_attn_out_proj_w': 6.07}
    for name, (base, spread) in spreads.items():
        noise = np.random.default_rng([zlib.crc32(name.encode()), seed]).standard_normal(out[name].shape)
        drawn = base * np.exp(spread * noise) if base else spread * noise
        out[name] = jnp.asarray(drawn.astype(out[name].dtype))
    for name, factor in factors.items():
        out[name] = (out[name] * factor).astype(out[name].dtype)
    return out
```

```python
from contextlib import ExitStack

import concourse.bass as bass
from concourse import mybir

F32 = mybir.dt.float32
BF16 = mybir.dt.bfloat16
I32 = mybir.dt.int32
ALU = mybir.AluOpType
ACT = mybir.ActivationFunctionType
AX = mybir.AxisListType

NB, S, H = 32, 128, 192
TOK = NB * S
KT, KP = 2, 96
NL, IN, NST, R, KC = 16, 384, 16, 48, 4
IB = IN // 128
CH = 512
CB = CH // S
NCH = TOK // CH
STEPS = NL * NCH
PAIRS = NST // 2
SLOTS = IB * PAIRS
EPS = 1e-5
SP, RR, ME, HD, GH = 8, 16, 64, 32, 64
TOPK = 4
TILES = CH // 128
EB = 4
NBLK = ME // EB


class Step:

    def __init__(self, it, s):
        self.it, self.s = it, s

    def plus(self, n):
        return Step(self.it, self.s + n)

    @property
    def parity(self):
        return self.s % 2

    def count(self, per, k):
        return self.it * (2 * per) + (self.s * per + k)

    def number(self):
        return self.it * 2 + self.s

    def tokens(self):
        return bass.ds((self.number() % NCH) * CH, CH)

    def layers(self, per):
        return (self.number() // NCH) * per + per


def need(eng, sem, value):
    if not isinstance(value, int) or value > 0:
        eng.wait_ge(sem, value)


def lm_tower(nc, ids, type_ids, tok_w, pos_w, type_w, gamma, beta, w_in, w_front, w_dt, w_back, a_log,
             final_w, p_w, c_blocks, w1, b1, w2, b2, g1, g1b, g2, g2b, h_scratch, out, steps=STEPS):
    ctx = ExitStack()
    with ctx:
        def sb(name, shape, dt=F32):
            return ctx.enter_context(nc.sbuf_tensor(name, shape, dt))

        def pb(name, shape):
            return ctx.enter_context(nc.psum_tensor(name, shape, F32))

        def sem(name):
            return ctx.enter_context(nc.semaphore(name))

        x_all = sb("x_all", [KP, KT, TOK])
        c_bc = sb("c_bc", [128, NST, CH])
        u_buf = sb("u_buf", [128, 2, IB, CH])
        z_buf = sb("z_buf", [128, 2, IB, CH])
        ndt = sb("ndt", [128, 2, IB, CH])
        dtu = sb("dtu", [128, 2, IB, CH])
        decay = sb("decay", [128, 3, 2, CB, S])
        state = sb("state", [128, 3, 2, CH])
        state_c = sb("state_c", [128, 3, 2, CH])
        exp_t = sb("exp_t", [128, IB, CH])
        rel_t = sb("rel_t", [128, IB, CH])
        xn = sb("xn", [KP, KT, CH])
        rs = sb("rs", [KP, CH])
        dtr = sb("dtr", [R, CH])
        bc3 = sb("bc3", [96, 2, CH], BF16)
        bc_mid = sb("bc_mid", [96, CH], BF16)
        bc_rest = sb("bc_rest", [96, CH])
        xsq = rel_t[0:KP, 0:KT, :]
        lns = bc_rest[0:KP, :]
        y_rows = sb("y_rows", [128, CH])
        gated = sb("gated", [128, IB, CH])
        sel = sb("sel", [96, 2 * NST, 128], BF16)
        ident = sb("ident", [128, 128])
        nident = sb("nident", [128, 128])
        win_x = sb("win", [128, KT * 2 * IN + KT])
        win = win_x[0:KP, :]
        wfr = sb("wfr", [128, IB * 96 + IB * (KC + 2)])
        wdt = sb("wdt", [R, IN])
        wbk = sb("wbk", [128, IB * H + IB])
        alog = sb("alog", [128, IB * NST])
        ea = sb("ea", [128, IB * NST])
        half = sb("half", [128, 1])
        epst = sb("epst", [128, 1])
        onesm = sb("onesm", [KP, KP])
        small = sb("small", [128, 6 * NB])

        w_in_v = win[:, 0:KT * 2 * IN].rearrange("p (k m) -> p k m", k=KT)
        nw_v = win[:, KT * 2 * IN:]
        w_x_v = wfr[:, 0:IB * 96].rearrange("p (k m) -> p k m", k=IB)
        o = IB * 96
        conv_w = wfr[:, o:o + IB * KC].rearrange("p (i k) -> p i k", i=IB)
        conv_b = wfr[:, o + IB * KC:o + IB * (KC + 1)]
        dt_b = wfr[:, o + IB * (KC + 1):o + IB * (KC + 2)]
        w_out_v = wbk[:, 0:IB * H].rearrange("p (k m) -> p k m", k=IB)
        d_v = wbk[:, IB * H:]

        b_bank = pb("b_bank", [128, 2, 2, CH])
        y_bank = pb("y_bank", [128, CH])
        c_bank = pb("c_bank", [128, CH])
        f_bank = pb("f_bank", [128, CH])
        k_bank = pb("k_bank", [128, CH])

        consts = sem("consts")
        dve_chain = sem("dve_chain")
        act_chain = sem("act_chain")
        pool_chain = sem("pool_chain")
        ids_in = sem("ids_in")
        tok_rows = [sem(f"tok_rows{i}") for i in range(4)]
        vec_in = sem("vec_in")
        centred = sem("centred")
        squared = sem("squared")
        var_ready = sem("var_ready")
        rstd_ready = sem("rstd_ready")
        h_ready = sem("h_ready")
        h_stored = sem("h_stored")
        x0_ready = sem("x0_ready")
        x0_turned = sem("x0_turned")
        x0_kept = sem("x0_kept")
        wf_in = sem("wf_in")
        wa_in = sem("wa_in")
        wb_in = sem("wb_in")
        b_full = sem("b_full")
        decay_full = sem("decay_full")
        drive_ready = sem("drive_ready")
        scan_done = sem("scan_done")
        cm_done = sem("cm_done")
        turned = sem("turned")
        c_full = sem("c_full")
        c_kept = sem("c_kept")
        ea_ready = sem("ea_ready")
        sq_ready = sem("sq_ready")
        f_full = sem("f_full")
        ln_ready = sem("ln_ready")
        rs_ready = sem("rs_ready")
        xr_ready = sem("xr_ready")
        xn_ready = sem("xn_ready")
        c0_ready = sem("c0_ready")
        tap_done = sem("tap_done")
        thu_ready = sem("thu_ready")
        u_ready = sem("u_ready")
        thz_ready = sem("thz_ready")
        z_ready = sem("z_ready")
        hi_ready = sem("hi_ready")
        rest_ready = sem("rest_ready")
        mid_ready = sem("mid_ready")
        parts_ready = sem("parts_ready")
        abs_ready = sem("abs_ready")
        rel_ready = sem("rel_ready")
        exp_ready = sem("exp_ready")
        ln1_ready = sem("ln1_ready")
        w1_ready = sem("w1_ready")
        ndt_ready = sem("ndt_ready")
        dtu_ready = sem("dtu_ready")
        y_kept = sem("y_kept")
        k_full = sem("k_full")
        x_ready = sem("x_ready")
        g_ready = sem("g_ready")
        gz_ready = sem("gz_ready")
        mix_open = sem("mix_open")
        mw_in = sem("mw_in")
        h_back = sem("h_back")
        xs_ready = sem("xs_ready")
        xt_full = sem("xt_full")
        xsq_ready = sem("xsq_ready")
        xss_ready = sem("xss_ready")
        xln_ready = sem("xln_ready")
        xrs_ready = sem("xrs_ready")
        hc_ready = sem("hc_ready")
        hsq_ready = sem("hsq_ready")
        hvar_ready = sem("hvar_ready")
        hln_ready = sem("hln_ready")
        hrs_ready = sem("hrs_ready")
        xf_ready = sem("xf_ready")
        xft_full = sem("xft_full")
        xft_ready = sem("xft_ready")
        zt_full = sem("zt_full")
        zt_ready = sem("zt_ready")
        sc_full = sem("sc_full")
        dif_ready = sem("dif_ready")
        exs_ready = sem("exs_ready")
        wt_ready = sem("wt_ready")
        wt_full = sem("wt_full")
        wt_kept = sem("wt_kept")
        whi_ready = sem("whi_ready")
        wrest_ready = sem("wrest_ready")
        wmid_ready = sem("wmid_ready")
        wlo_ready = sem("wlo_ready")
        h1_full = sem("h1_full")
        gelu_done = sem("gelu_done")
        gate_full = sem("gate_full")
        hg_ready = sem("hg_ready")
        hg_used = sem("hg_used")
        comb_ready = sem("comb_ready")
        g1_full = sem("g1_full")
        g1_ready = sem("g1_ready")
        o_full = sem("o_full")
        o_ready = sem("o_ready")
        mchain = sem("mchain")
        out_done = sem("out_done")

        FUSES = 14
        KUSES = IB + KT

        block = ctx.enter_context(nc.Block())

        def steps_loop(eng, step):
            step(Step(0, 0), first=True)
            step(Step(0, 1))
            if steps > 4:
                with eng.Fori(1, steps // 2 - 1) as it:
                    step(Step(it, 0))
                    step(Step(it, 1))
            step(Step(0, steps - 2))
            step(Step(0, steps - 1), front=False)

        GR = 4
        GB = NB // GR
        emb = c_bc[:, :, :].rearrange("p a b -> p (a b)")[:, 0:NB * H].rearrange("p (b h) -> p b h", b=NB)
        typ = u_buf[:, :, :, :].rearrange("p a i t -> p (a i t)")
        typ2 = z_buf[:, :, :, :].rearrange("p a i t -> p (a i t)")
        typ_g = [(typ, typ2)[g // 2][:, (g % 2) * GB * H:(g % 2 + 1) * GB * H].rearrange(
            "p (b h) -> p b h", b=GB) for g in range(GR)]
        sq_g = ndt[:, :, :, :].rearrange("p a i t -> p (a i t)")[:, 0:GB * H].rearrange("p (b h) -> p b h", b=GB)
        x0_g = [dtu[:, :, :, :].rearrange("p a i t -> p (a i t)")[:, g * GB * H:(g + 1) * GB * H].rearrange(
            "p (b h) -> p b h", b=GB) for g in range(2)]
        vecs = exp_t[:, :, :].rearrange("p a b -> p (a b)")
        pos_v, gam_v, bet_v = (vecs[:, i * H:(i + 1) * H] for i in range(3))
        id_v = y_rows[:, 0:2 * NB].bitcast(I32)
        st_sum, st_mean, st_var, st_ln, st_rstd = (small[:, i * GB:(i + 1) * GB] for i in range(5))

        def flat(t):
            return t.rearrange("p a i t -> p (a i t)")

        uf, zf, nf, df = (flat(t[:, :, :, :]) for t in (u_buf, z_buf, ndt, dtu))
        sf, scf = flat(state[:, :, :, :]), flat(state_c[:, :, :, :])
        dcf = decay[:, :, :, :, :].rearrange("p r a b t -> p (r a b t)")
        cf = c_bc[:, :, :].rearrange("p a b -> p (a b)")
        NW1 = 2 * ME * HD
        w1_v = cf[:, 0:NW1]
        w2_v = cf[:, NW1:2 * NW1].rearrange("p (b m) -> p b m", m=2 * RR)
        gsel = uf[:, 0:2048].bitcast(BF16).rearrange("p (b m) -> p b m", m=128)
        cb_v = uf[:, 2048:2560]
        p_v = uf[0:KP, 2560:2816].rearrange("p (k m) -> p k m", k=KT)
        b1_v = uf[:, 2816:2944]
        b2_v = uf[:, 2944:3072].rearrange("p (s m) -> p s m", m=2 * RR)
        g1_v, g1b_v = wfr[:, 0:GH], wfr[0:GH, GH:GH + 1]
        fw_v, g2_v = wbk[:, 0:H], wbk[0:GH + 1, H:2 * H]

        def tiles(v):
            return v.rearrange("p (t h) -> p t h", t=TILES)

        h_in, h2, xf, sqm = (tiles(zf[:, i * TILES * H:(i + 1) * TILES * H]) for i in range(4))
        xs = exp_t[0:KP, 0:KT, :]
        xf_t = nf[0:KP, 0:KT * CH].rearrange("p (k t) -> p k t", k=KT)
        z_t, comb, g1o = (nf[:, i * CH:(i + 1) * CH] for i in (2, 3, 4))
        rep, dif, exs, wt = (df[:, i * CH:(i + 1) * CH] for i in range(4))
        wt32 = sf[:, 0:4 * CH].rearrange("p (s t) -> p s t", s=4)
        wrest = dcf[:, 0:4 * CH].rearrange("p (s t) -> p s t", s=4)
        w_parts = [cfx.bitcast(BF16).rearrange("p (s t) -> p s t", s=4)
                   for cfx in (dcf[:, 2048:3072], sf[:, 2048:3072], win_x[:, 0:1024])]
        hid = scf.rearrange("p (r t) -> p r t", t=CH)
        sm_ss, sm_ln, sm_rs, sm_sum, sm_mean, sm_var, sm_vln, sm_rstd = (small[:, 4 * i:4 * i + 4] for i in range(8))
        top8 = small[:, 32:96].rearrange("p (s k) -> p s k", s=SP)
        top4 = small[:, 96:160].rearrange("p (s k) -> p s k", s=SP)
        den, rden = small[:, 160:168], small[:, 168:176]
        xt_p = b_bank[:, 0, :, 0:2 * H].rearrange("p a (b h) -> p a b h", b=2)
        xft_p = b_bank[0:KP, 1, :, :]
        sc_p = (f_bank, k_bank)
        h1_p, gate_p = (b_bank[:, i, :, :] for i in range(2))
        LOW = -3.0e38

        @block.sync
        def _(sp):
            sp.dma_start(id_v[:, 0:NB], ids).then_inc(ids_in, 16)
            sp.dma_start(id_v[:, NB:2 * NB], type_ids).then_inc(ids_in, 16)
            sp.dma_start(pos_v, pos_w).then_inc(vec_in, 16)
            sp.dma_start(gam_v, gamma.partition_broadcast(128)).then_inc(vec_in, 16)
            sp.dma_start(bet_v, beta.partition_broadcast(128)).then_inc(vec_in, 16)

            def load_layer(layer):
                first = layer * NCH
                if not isinstance(first, int) or first > 0:
                    sp.wait_ge(dtu_ready, first * IB)
                sp.dma_start(win[:, :], w_in[bass.ds(layer, 1)].rearrange("a p m -> (a p) m")).then_inc(wf_in, 16)
                sp.dma_start(wfr[:, :], w_front[bass.ds(layer, 1)].rearrange("a p m -> (a p) m")).then_inc(wf_in, 16)
                sp.dma_start(wdt[:, :], w_dt[bass.ds(layer, 1)].rearrange("a p m -> (a p) m")).then_inc(wf_in, 16)
                if not isinstance(first, int) or first > 0:
                    sp.wait_ge(ea_ready, first)
                sp.dma_start(alog[:, :], a_log[bass.ds(layer, 1)].rearrange("a p m -> (a p) m")).then_inc(wa_in, 16)
                if not isinstance(first, int) or first > 0:
                    sp.wait_ge(x_ready, first * KT)
                sp.dma_start(wbk[:, :], w_back[bass.ds(layer, 1)].rearrange("a p m -> (a p) m")).then_inc(wb_in, 16)

            nl = (steps + NCH - 1) // NCH
            load_layer(0)
            for g in range(GR):
                sp.wait_ge(h_ready, g + 1)
                sp.dma_start(h_scratch[:, g * GB:(g + 1) * GB, :], emb[:, g * GB:(g + 1) * GB, :]).then_inc(h_stored, 16)
            if nl > 1:
                with sp.Fori(1, nl) as layer:
                    load_layer(layer)
            sp.wait_ge(h_stored, 16 * GR)

            sp.wait_ge(mix_open, 1)
            for dst, src in ((w1_v, w1), (w2_v, w2), (cb_v, c_blocks), (p_v, p_w), (b1_v, b1), (b2_v, b2),
                             (g1_v, g1), (g1b_v, g1b), (fw_v, final_w.partition_broadcast(128)),
                             (g2_v[0:GH, :], g2), (g2_v[GH:GH + 1, :], g2b.rearrange("(a h) -> a h", a=1))):
                sp.dma_start(dst, src).then_inc(mw_in, 16)
            with sp.Fori(0, NCH) as c:
                sp.wait_ge(mix_open, c + 1)
                sp.dma_start(h_in, h_scratch[:, bass.ds(c * CB, CB), :]).then_inc(h_back, 16)
                sp.wait_ge(o_ready, c + 1)
                sp.dma_start(out[bass.ds(c * CB, CB), :, :].rearrange("b s h -> s b h"), xf).then_inc(out_done, 16)
            sp.wait_ge(out_done, 16 * NCH)

        @block.gpsimd
        def _(pool):
            pool.memset(ident[:, :], 0.0).then_inc(pool_chain, 1)
            pool.memset(nident[:, :], 0.0).then_inc(pool_chain, 1)
            pool.memset(sel[:, :, :], 0.0).then_inc(pool_chain, 1)
            pool.memset(half[:, :], 0.5).then_inc(pool_chain, 1)
            pool.memset(epst[:, :], EPS).then_inc(consts, 1)
            pool.memset(onesm[:, :], 1.0).then_inc(consts, 1)
            pool.memset(decay[:, :, :, :, 0:1], 0.0).then_inc(consts, 1)
            pool.wait_ge(pool_chain, 4)
            for m, fill in ((ident, 1.0), (nident, -1.0)):
                pool.affine_select(out=m[:, :], in_=m[:, :], compare_op=ALU.not_equal, fill=fill, base=0,
                                   pattern=[[-1, 128]], channel_multiplier=1).then_inc(consts, 1)
            pool.wait_ge(consts, 5)
            pool.memset(half[64:64 + NST, :], 0.25).then_inc(consts, 1)
            for part in range(3):
                pool.wait_ge(consts, 6 + part)
                pool.affine_select(out=sel[32 * part:32 * part + 32, :, :], in_=sel[32 * part:32 * part + 32, :, :],
                                   compare_op=ALU.not_equal, fill=1.0, base=0,
                                   pattern=[[-1, 2 * NST], [0, 128]], channel_multiplier=1).then_inc(consts, 1)
            pool.wait_ge(consts, 9)
            pool.wait_ge(ids_in, 32)
            for b in range(NB):
                g = b // GB
                pool.indirect_dma_start(emb[:, b, :], None, tok_w, bass.IndirectOffsetOnAxis(id_v[:, b:b + 1], 0)
                                        ).then_inc(tok_rows[g], 16)
                pool.indirect_dma_start(typ_g[g][:, b % GB, :], None, type_w,
                                        bass.IndirectOffsetOnAxis(id_v[:, NB + b:NB + b + 1], 0)
                                        ).then_inc(tok_rows[g], 16)

            def norm(fi):
                pool.wait_ge(rs_ready, fi.count(1, 1))
                pool.wait_ge(wf_in, fi.layers(48))
                pool.tensor_tensor(xn[:, :, :], x_all[:, :, fi.tokens()],
                                   rs[:, :].unsqueeze(1).to_broadcast([KP, KT, CH]), ALU.mult).then_inc(xr_ready, 1)
                pool.wait_ge(xr_ready, fi.count(1, 1))
                pool.tensor_tensor(xn[:, :, :], xn[:, :, :], nw_v.unsqueeze(2).to_broadcast([KP, KT, CH]), ALU.mult
                                   ).then_inc(xn_ready, 1)

            def times_c(g, j):
                pool.wait_ge(scan_done, g.count(SLOTS, j + 1))
                if j < PAIRS:
                    pool.wait_ge(c_kept, g.count(NST, 2 * j + 2))
                need(pool, turned, g.count(SLOTS, j - 2))
                q = j % PAIRS
                pool.tensor_tensor(state_c[:, j % 3, :, :], state[:, j % 3, :, :], c_bc[:, 2 * q:2 * q + 2, :],
                                   ALU.mult).then_inc(cm_done, 1)

            def gate_z(g, i):
                pool.wait_ge(g_ready, g.count(IB, i + 1))
                if i == 0:
                    pool.wait_ge(z_ready, g.count(IB, IB))
                pool.tensor_tensor(gated[:, i, :], gated[:, i, :], z_buf[:, g.parity, i, :], ALU.mult
                                   ).then_inc(gz_ready, 1)

            def step(g, first=False, front=True):
                for j in range(SLOTS):
                    times_c(g, j)
                    if j == 3 and front:
                        norm(g.plus(1))
                    if j == 4 and not first:
                        gate_z(g.plus(-1), 2)
                    if j in (12, 20):
                        gate_z(g, (j - 12) // 8)

            norm(Step(0, 0))
            steps_loop(pool, step)
            gate_z(Step(0, steps - 1), 2)

        @block.scalar
        def _(act):
            act.wait_ge(consts, 9)
            for g in range(GR):
                for half_ln in range(2):
                    k = 2 * g + half_ln
                    act.wait_ge(centred, k + 1)
                    act.activation(sq_g, (emb[:, g * GB:(g + 1) * GB, :], x0_g[g % 2])[half_ln], ACT.Square
                                   ).then_inc(squared, 1)
                    act.wait_ge(var_ready, k + 1)
                    act.activation(st_ln, st_var, ACT.Ln, bias=epst[:, 0:1], scale=1.0 / H).then_inc(act_chain, 1)
                    act.wait_ge(act_chain, k + 1)
                    act.activation(st_rstd, st_ln, ACT.Exp, scale=-0.5).then_inc(rstd_ready, 1)
                for t in range(GB // CB):
                    for k in range(KT):
                        n = (g * (GB // CB) + t) * KT + k
                        act.wait_ge(x0_turned, n + 1)
                        c = g * (GB // CB) + t
                        act.activation(x_all[:, k, c * CH:(c + 1) * CH], (f_bank, k_bank)[k][0:KP, :], ACT.Copy
                                       ).then_inc(x0_kept, 1)

            def square(fi, g=None):
                if g is None:
                    act.wait_ge(x0_kept, 2 * NCH)
                else:
                    need(act, x_ready, g.count(KT, -KT))
                need(act, f_full, fi.count(FUSES, 0))
                act.activation(xsq[:, :, :], x_all[:, :, fi.tokens()], ACT.Square).then_inc(sq_ready, 1)

            def inverse_rms(fi):
                act.wait_ge(f_full, fi.count(FUSES, 1))
                act.activation(lns[:, :], f_bank[0:KP, :], ACT.Ln, bias=epst[0:KP, 0:1], scale=1.0 / H
                               ).then_inc(ln_ready, 1)
                act.wait_ge(ln_ready, fi.count(1, 1))
                act.activation(rs[:, :], lns[:, :], ACT.Exp, scale=-0.5).then_inc(rs_ready, 1)

            def conv_first(fi, m):
                act.wait_ge(f_full, fi.count(FUSES, 2 + m))
                need(act, g_ready, fi.count(IB, -IB))
                act.activation(u_buf[:, fi.parity, m, :], f_bank[:, :], ACT.Identity,
                               scale=conv_w[:, m, KC - 1:KC], bias=conv_b[:, m:m + 1]).then_inc(c0_ready, 1)

            def tanh_u(fi, m):
                act.wait_ge(tap_done, fi.count(IB * (KC - 1), (m + 1) * (KC - 1)))
                act.activation(exp_t[:, m, :], u_buf[:, fi.parity, m, :], ACT.Tanh, scale=0.5).then_inc(thu_ready, 1)

            def tanh_z(fi, m):
                act.wait_ge(f_full, fi.count(FUSES, 5 + m))
                need(act, gz_ready, fi.count(IB, -IB))
                act.activation(z_buf[:, fi.parity, m, :], f_bank[:, :], ACT.Tanh, scale=0.5).then_inc(thz_ready, 1)

            def take_x_proj(fi):
                act.wait_ge(f_full, fi.count(FUSES, 8))
                act.activation(dtr[:, :], f_bank[0:R, :], ACT.Copy, scale=0.5).then_inc(hi_ready, 1)
                act.activation(bc3[64:96, fi.parity, :], f_bank[64:96, :], ACT.Copy, scale=half[64:96, 0:1]
                               ).then_inc(hi_ready, 1)

            def middle(fi):
                act.wait_ge(rest_ready, fi.count(1, 1))
                act.activation(bc_mid[64:96, :], bc_rest[64:96, :], ACT.Copy).then_inc(mid_ready, 1)
                act.wait_ge(mid_ready, fi.count(1, 1))
                act.activation(bc3[32:64, fi.parity, :], bc_mid[64:96, :], ACT.Copy).then_inc(parts_ready, 1)

            def abs_relu(fi, m):
                act.wait_ge(f_full, fi.count(FUSES, 9 + m))
                act.wait_ge(u_ready, fi.count(IB, IB))
                act.activation(exp_t[:, m, :], f_bank[:, :], ACT.Abs, bias=dt_b[:, m:m + 1]).then_inc(abs_ready, 1)
                act.activation(rel_t[:, m, :], f_bank[:, :], ACT.Relu, bias=dt_b[:, m:m + 1]).then_inc(rel_ready, 1)

            def soft(fi):
                act.wait_ge(abs_ready, fi.count(IB, IB))
                act.activation(exp_t[:, :, :], exp_t[:, :, :], ACT.Exp, scale=-1.0).then_inc(exp_ready, 1)
                act.wait_ge(exp_ready, fi.count(1, 1))
                act.activation(ndt[:, fi.parity, :, :], exp_t[:, :, :], ACT.Ln, bias=1.0).then_inc(ln1_ready, 1)

            def take_ndt(fi, m):
                act.wait_ge(f_full, fi.count(FUSES, 12 + m))
                act.activation(ndt[:, fi.parity, m, :], f_bank[:, :], ACT.Copy, scale=-1.0).then_inc(ndt_ready, 1)

            def take_a(fi):
                act.wait_ge(wa_in, fi.layers(16))
                act.activation(ea[:, :], alog[:, :], ACT.Exp).then_inc(ea_ready, 1)

            def decays(g, j):
                i, q = divmod(j, PAIRS)
                if j % PAIRS == 0:
                    act.wait_ge(ndt_ready, g.count(IB, i + 1))
                if j == 0:
                    act.wait_ge(ea_ready, g.count(1, 1))
                need(act, scan_done, g.count(SLOTS, j - 2))
                nd = ndt[:, g.parity, i, :].rearrange("p (b t) -> p b t", b=CB)
                for k in range(2):
                    n = i * NST + 2 * q + k
                    act.activation(decay[:, j % 3, k, :, 1:S], nd[:, :, 1:S], ACT.Exp, scale=ea[:, n:n + 1]
                                   ).then_inc(decay_full, 1)

            def keep_c(g, q):
                for k in range(2):
                    act.wait_ge(c_full, g.count(NST, 2 * q + k + 1))
                    if k == 0:
                        need(act, cm_done, g.count(SLOTS, q - 7))
                    act.activation(c_bc[:, 2 * q + k, :], c_bank[:, :], ACT.Copy).then_inc(c_kept, 1)

            def keep_y(g, i):
                act.wait_ge(turned, g.count(SLOTS, PAIRS * (i + 1)))
                need(act, k_full, g.count(KUSES, i - (2 if i == 0 else 0)))
                act.activation(y_rows[:, :], y_bank[:, :], ACT.Copy, scale=2.0).then_inc(y_kept, 1)

            def step(g, first=False, front=True):
                f = g.plus(1)
                for j in range(SLOTS):
                    if j + 2 < SLOTS:
                        decays(g, j + 2)
                    elif front:
                        decays(f, j + 2 - SLOTS)
                    if j < 2:
                        keep_c(g, 6 + j)
                    if j >= 18 and front:
                        keep_c(f, j - 18)
                    if j == 1 and not first:
                        keep_y(g.plus(-1), 2)
                    if j in (9, 17):
                        keep_y(g, (j - 9) // 8)
                    if not front:
                        continue
                    if j == 0:
                        square(f, g)
                    if j == 2:
                        inverse_rms(f)
                    if j in (4, 6, 8):
                        conv_first(f, (j - 4) // 2)
                    if j in (7, 9, 11):
                        tanh_u(f, (j - 7) // 2)
                    if j in (10, 11, 12):
                        tanh_z(f, j - 10)
                    if j == 13:
                        take_x_proj(f)
                    if j == 15:
                        middle(f)
                    if j in (15, 16, 17):
                        abs_relu(f, j - 15)
                    if j == 18:
                        soft(f)
                    if j in (20, 21, 22):
                        take_ndt(f, j - 20)
                    if j == 21:
                        take_a(f)

            p = Step(0, 0)
            square(p)
            inverse_rms(p)
            for m in range(IB):
                conv_first(p, m)
                tanh_u(p, m)
            for m in range(IB):
                tanh_z(p, m)
            take_x_proj(p)
            middle(p)
            for m in range(IB):
                abs_relu(p, m)
            soft(p)
            take_a(p)
            for m in range(IB):
                take_ndt(p, m)
            act.wait_ge(h_stored, 16 * GR)
            for q in range(6):
                keep_c(p, q)
            decays(p, 0)
            decays(p, 1)
            steps_loop(act, step)
            keep_y(Step(0, steps - 1), 2)

            with act.Fori(0, NCH) as c:
                act.wait_ge(mix_open, c + 1)
                act.activation(xs, x_all[:, :, bass.ds(c * CH, CH)], ACT.Copy).then_inc(xs_ready, 1)
                act.wait_ge(xt_full, c + 1)
                act.activation(sqm.rearrange("p (a b) h -> p a b h", a=2), xt_p, ACT.Square).then_inc(xsq_ready, 1)
                act.wait_ge(xss_ready, c + 1)
                act.activation(sm_ln, sm_ss, ACT.Ln, bias=epst[:, 0:1], scale=1.0 / H).then_inc(xln_ready, 1)
                act.wait_ge(xln_ready, c + 1)
                act.activation(sm_rs, sm_ln, ACT.Exp, scale=-0.5).then_inc(xrs_ready, 1)
                act.wait_ge(hc_ready, c + 1)
                act.activation(sqm, xf, ACT.Square).then_inc(hsq_ready, 1)
                act.wait_ge(hvar_ready, c + 1)
                act.activation(sm_vln, sm_var, ACT.Ln, bias=epst[:, 0:1], scale=1.0 / H).then_inc(hln_ready, 1)
                act.wait_ge(hln_ready, c + 1)
                act.activation(sm_rstd, sm_vln, ACT.Exp, scale=-0.5).then_inc(hrs_ready, 1)
                act.wait_ge(xft_full, c + 1)
                act.activation(xf_t, xft_p, ACT.Copy).then_inc(xft_ready, 1)
                act.wait_ge(zt_full, c + 1)
                act.activation(z_t, y_bank[:, :], ACT.Copy).then_inc(zt_ready, 1)
                for t in range(TILES):
                    act.wait_ge(dif_ready, c * TILES + (t + 1))
                    act.activation(exs, dif, ACT.Exp).then_inc(exs_ready, 1)
                    act.wait_ge(wt_full, c * TILES + (t + 1))
                    act.activation(wt32[:, :, t * 128:(t + 1) * 128],
                                   c_bank[:, :].rearrange("p (s t) -> p s t", s=4), ACT.Copy).then_inc(wt_kept, 1)
                act.wait_ge(wt_kept, c * TILES + TILES)
                act.activation(w_parts[0], wt32, ACT.Copy).then_inc(whi_ready, 1)
                act.wait_ge(wrest_ready, c + 1)
                act.activation(w_parts[1], wrest, ACT.Copy).then_inc(wmid_ready, 1)
                for b in range(SP * NBLK):
                    act.wait_ge(h1_full, c * (SP * NBLK) + (b + 1))
                    if b >= 3:
                        act.wait_ge(hg_ready, c * (SP * NBLK) + (b - 2))
                    act.activation(hid[:, b % 3, :], h1_p[:, b % 2, :], ACT.Gelu_apprx_tanh, bias=b1_v[:, b:b + 1]
                                   ).then_inc(gelu_done, 1)
                act.wait_ge(hg_used, c * (SP * NBLK) + SP * NBLK)
                act.activation(comb, y_bank[:, :], ACT.Copy).then_inc(comb_ready, 1)
                act.wait_ge(g1_full, c + 1)
                act.activation(g1o[0:GH, :], f_bank[0:GH, :], ACT.Gelu_apprx_tanh, bias=g1b_v).then_inc(g1_ready, 1)

        @block.vector
        def _(dve):
            chain = [0]

            def link(ins):
                chain[0] += 1
                ins.then_inc(dve_chain, 1)
                dve.wait_ge(dve_chain, chain[0])

            def layer_norm(src, dst, k):
                link(dve.tensor_reduce(st_sum, src, AX.X, ALU.add))
                link(dve.tensor_scalar(st_mean, st_sum, 1.0 / H, None, ALU.mult))
                dve.tensor_tensor(dst, src, st_mean.unsqueeze(2).to_broadcast([128, GB, H]), ALU.subtract
                                  ).then_inc(centred, 1)
                dve.wait_ge(squared, k + 1)
                dve.tensor_reduce(st_var, sq_g, AX.X, ALU.add).then_inc(var_ready, 1)
                dve.wait_ge(rstd_ready, k + 1)
                return dve.tensor_tensor(dst, dst, st_rstd.unsqueeze(2).to_broadcast([128, GB, H]), ALU.mult)

            dve.wait_ge(vec_in, 48)
            for g in range(GR):
                e = emb[:, g * GB:(g + 1) * GB, :]
                dve.wait_ge(tok_rows[g], 32 * GB)
                link(dve.tensor_tensor(e, e, pos_v.unsqueeze(1).to_broadcast([128, GB, H]), ALU.add))
                link(dve.tensor_tensor(e, e, typ_g[g], ALU.add))
                link(layer_norm(e, e, 2 * g))
                link(dve.tensor_tensor(e, e, gam_v.unsqueeze(1).to_broadcast([128, GB, H]), ALU.mult))
                link2 = dve.tensor_tensor(e, e, bet_v.unsqueeze(1).to_broadcast([128, GB, H]), ALU.add)
                link2.then_inc(h_ready, 1)
                dve.wait_ge(h_ready, g + 1)
                if g >= 2:
                    dve.wait_ge(x0_turned, (g - 1) * (GB // CB) * KT)
                layer_norm(e, x0_g[g % 2], 2 * g + 1).then_inc(x0_ready, 1)

            def tap(fi, m, k):
                u = u_buf[:, fi.parity, m, :].rearrange("p (b t) -> p b t", b=CB)
                f = f_bank[:, :].rearrange("p (b t) -> p b t", b=CB)
                if k == 1:
                    dve.wait_ge(c0_ready, fi.count(IB, m + 1))
                else:
                    dve.wait_ge(tap_done, fi.count(IB * (KC - 1), m * (KC - 1) + k - 1))
                ins = dve.scalar_tensor_tensor(out=u[:, :, k:S], in0=f[:, :, 0:S - k],
                                               scalar=conv_w[:, m, KC - 1 - k:KC - k], in1=u[:, :, k:S],
                                               op0=ALU.mult, op1=ALU.add)
                ins.then_inc(tap_done, 1)

            def silu_u(fi, m):
                dve.wait_ge(thu_ready, fi.count(IB, m + 1))
                u = u_buf[:, fi.parity, m, :]
                dve.scalar_tensor_tensor(out=u, in0=exp_t[:, m, :], scalar=1.0, in1=u, op0=ALU.add, op1=ALU.mult
                                         ).then_inc(u_ready, 1)

            def silu_z(fi, m):
                dve.wait_ge(thz_ready, fi.count(IB, m + 1))
                z = z_buf[:, fi.parity, m, :]
                dve.scalar_tensor_tensor(out=z, in0=z, scalar=1.0, in1=f_bank[:, :], op0=ALU.add, op1=ALU.mult
                                         ).then_inc(z_ready, 1)

            def rest(fi):
                dve.wait_ge(hi_ready, fi.count(2, 2))
                dve.scalar_tensor_tensor(out=bc_rest[64:96, :], in0=f_bank[64:96, :], scalar=half[64:96, 0:1],
                                         in1=bc3[64:96, fi.parity, :], op0=ALU.mult, op1=ALU.subtract
                                         ).then_inc(rest_ready, 1)

            def lowest(fi):
                dve.wait_ge(mid_ready, fi.count(1, 1))
                dve.tensor_tensor(bc3[0:32, fi.parity, :], bc_rest[64:96, :], bc_mid[64:96, :], ALU.subtract
                                  ).then_inc(parts_ready, 1)

            def one_less(fi):
                dve.wait_ge(exp_ready, fi.count(1, 1))
                dve.tensor_scalar(dtu[:, fi.parity, :, :], exp_t[:, :, :], 1.0, -1.0, ALU.add, ALU.add
                                  ).then_inc(w1_ready, 1)

            def take_dtu(fi, m):
                dve.wait_ge(ndt_ready, fi.count(IB, m + 1))
                dve.tensor_tensor(dtu[:, fi.parity, m, :], u_buf[:, fi.parity, m, :], f_bank[:, :], ALU.mult
                                  ).then_inc(dtu_ready, 1)

            def drive(g, j):
                i = j // PAIRS
                dve.wait_ge(b_full, g.count(SLOTS, j + 1))
                if j % PAIRS == 0:
                    dve.wait_ge(dtu_ready, g.count(IB, i + 1))
                b = b_bank[:, j % 2, :, :]
                dve.tensor_tensor(b, dtu[:, g.parity, i, :].unsqueeze(1).to_broadcast([128, 2, CH]), b, ALU.mult
                                  ).then_inc(drive_ready, 1)

            def scan(g, j):
                dve.wait_ge(drive_ready, g.count(SLOTS, j + 1))
                dve.wait_ge(decay_full, g.count(2 * SLOTS, 2 * j + 2))
                need(dve, cm_done, g.count(SLOTS, j - 2))
                dve.tensor_tensor_scan(state[:, j % 3, :, :].rearrange("p a t -> p (a t)"),
                                       decay[:, j % 3, :, :, :].rearrange("p a b t -> p (a b t)"),
                                       b_bank[:, j % 2, :, :].rearrange("p a t -> p (a t)"),
                                       0.0, ALU.mult, ALU.add).then_inc(scan_done, 1)

            def gate_d(g, i):
                dve.wait_ge(k_full, g.count(KUSES, i + 1))
                if i == 0:
                    dve.wait_ge(wb_in, g.layers(16))
                dve.scalar_tensor_tensor(out=gated[:, i, :], in0=u_buf[:, g.parity, i, :], scalar=d_v[:, i:i + 1],
                                         in1=k_bank[:, :], op0=ALU.mult, op1=ALU.add).then_inc(g_ready, 1)

            def residual(g, k):
                dve.wait_ge(k_full, g.count(KUSES, IB + 1 + k))
                x = x_all[:, k, g.tokens()]
                dve.scalar_tensor_tensor(out=x, in0=k_bank[0:KP, :], scalar=0.25, in1=x,
                                         op0=ALU.mult, op1=ALU.add).then_inc(x_ready, 1)

            def step(g, first=False, front=True):
                f = g.plus(1)
                for j in range(SLOTS):
                    drive(g, j)
                    if front and j in (5, 7, 9):
                        tap(f, (j - 5) // 2, 1)
                    if front and j in (6, 8, 10):
                        tap(f, (j - 6) // 2, 3)
                    if front and j in (11, 12, 13):
                        silu_z(f, j - 11)
                    if front and j == 14:
                        rest(f)
                    if front and j == 16:
                        lowest(f)
                    if front and j == 19:
                        one_less(f)
                    scan(g, j)
                    if front and j in (5, 7, 9):
                        tap(f, (j - 5) // 2, 2)
                    if front and j in (8, 10, 12):
                        silu_u(f, (j - 8) // 2)
                    if front and j in (21, 22, 23):
                        take_dtu(f, j - 21)
                    if j == 3 and not first:
                        gate_d(g.plus(-1), 2)
                    if j in (6, 7) and not first:
                        residual(g.plus(-1), j - 6)
                    if j in (11, 19):
                        gate_d(g, (j - 11) // 8)

            p = Step(0, 0)
            for m in range(IB):
                for k in range(1, KC):
                    tap(p, m, k)
                silu_u(p, m)
            for m in range(IB):
                silu_z(p, m)
            rest(p)
            lowest(p)
            one_less(p)
            for m in range(IB):
                take_dtu(p, m)
            steps_loop(dve, step)
            last = Step(0, steps - 1)
            gate_d(last, 2)
            residual(last, 0)
            residual(last, 1)

            dve.wait_ge(x_ready, steps * KT)
            dve.tensor_copy(gsel.rearrange("p b (m h) -> p (b m) h", h=HD),
                            ident[:, :].unsqueeze(2).to_broadcast([128, 128, HD])).then_inc(mchain, 1)
            dve.memset(top4, LOW).then_inc(mchain, 1)
            dve.memset(g1o[GH:GH + 1, :], 1.0).then_inc(mchain, 1)
            dve.wait_ge(mchain, 3)
            dve.sem_inc(mix_open, 1)
            MC = 3
            ML = 5 + TILES * 7

            def bc(v):
                return v.unsqueeze(2).to_broadcast([128, TILES, H])

            def apart():
                dve.memset(small[:, 176:177], 0.0)

            dve.wait_ge(mw_in, 16 * 11)
            with dve.Fori(0, NCH) as c:
                at = [0]

                def mlink(ins):
                    at[0] += 1
                    ins.then_inc(mchain, 1)
                    dve.wait_ge(mchain, c * ML + (MC + at[0]))

                dve.wait_ge(xsq_ready, c + 1)
                dve.tensor_reduce(sm_ss, sqm, AX.X, ALU.add).then_inc(xss_ready, 1)
                dve.wait_ge(xrs_ready, c + 1)
                mlink(dve.tensor_tensor(h2.rearrange("p (a b) h -> p a b h", a=2), xt_p,
                                        sm_rs.rearrange("p (a b) -> p a b", a=2).unsqueeze(3).to_broadcast([128, 2, 2, H]),
                                        ALU.mult))
                mlink(dve.tensor_tensor(h2, h2, fw_v.unsqueeze(1).to_broadcast([128, TILES, H]), ALU.mult))
                dve.wait_ge(h_back, c * 16 + 16)
                mlink(dve.tensor_tensor(h2, h2, h_in, ALU.add))
                mlink(dve.tensor_reduce(sm_sum, h2, AX.X, ALU.add))
                mlink(dve.tensor_scalar(sm_mean, sm_sum, 1.0 / H, None, ALU.mult))
                dve.wait_ge(out_done, c * 16)
                dve.tensor_tensor(xf, h2, bc(sm_mean), ALU.subtract).then_inc(hc_ready, 1)
                dve.wait_ge(hsq_ready, c + 1)
                dve.tensor_reduce(sm_var, sqm, AX.X, ALU.add).then_inc(hvar_ready, 1)
                dve.wait_ge(hrs_ready, c + 1)
                dve.tensor_tensor(xf, xf, bc(sm_rstd), ALU.mult).then_inc(xf_ready, 1)
                for t in range(TILES):
                    p = sc_p[t % 2][:, :]
                    p3 = p.rearrange("p (s m) -> p s m", s=SP)
                    dve.wait_ge(sc_full, c * TILES + (t + 1))
                    apart()
                    for s in range(SP):
                        ins = dve.max(top8[:, s, :], p3[:, s, :])
                    mlink(ins)
                    mlink(dve.tensor_copy(top4[:, :, 0:TOPK], top8[:, :, 0:TOPK]))
                    apart()
                    for s in range(SP):
                        ins = dve.match_replace(rep[:, s * ME:(s + 1) * ME], top4[:, s, :], p3[:, s, :], LOW)
                    dve.tensor_tensor(dif.rearrange("p (s m) -> p s m", s=SP), p3,
                                      top8[:, :, 0:1].to_broadcast([128, SP, ME]), ALU.subtract).then_inc(dif_ready, 1)
                    mlink(ins)
                    mlink(dve.tensor_tensor(rep, p, rep, ALU.not_equal))
                    dve.wait_ge(exs_ready, c * TILES + (t + 1))
                    mlink(dve.tensor_tensor(exs, exs, rep, ALU.mult))
                    mlink(dve.tensor_reduce(den, exs.rearrange("p (s m) -> p s m", s=SP), AX.X, ALU.add))
                    mlink(dve.reciprocal(rden, den))
                    dve.tensor_tensor(wt.rearrange("p (s m) -> p s m", s=SP), exs.rearrange("p (s m) -> p s m", s=SP),
                                      rden.unsqueeze(2).to_broadcast([128, SP, ME]), ALU.mult).then_inc(wt_ready, 1)
                dve.wait_ge(whi_ready, c + 1)
                dve.tensor_tensor(wrest, wt32, w_parts[0], ALU.subtract).then_inc(wrest_ready, 1)
                dve.wait_ge(wmid_ready, c + 1)
                dve.tensor_tensor(w_parts[2], wrest, w_parts[1], ALU.subtract).then_inc(wlo_ready, 1)
                for b in range(SP * NBLK):
                    dve.wait_ge(gelu_done, c * (SP * NBLK) + (b + 1))
                    dve.wait_ge(gate_full, c * (SP * NBLK) + (b + 1))
                    if b >= 3:
                        dve.wait_ge(hg_used, c * (SP * NBLK) + (b - 2))
                    dve.tensor_tensor(hid[:, 3 + b % 3, :], hid[:, b % 3, :], gate_p[:, b % 2, :], ALU.mult
                                      ).then_inc(hg_ready, 1)
                dve.wait_ge(o_full, c + 1)
                dve.tensor_tensor(xf.rearrange("p (a b) h -> p a b h", a=2), xt_p,
                                  h2.rearrange("p (a b) h -> p a b h", a=2), ALU.add).then_inc(o_ready, 1)
                dve.wait_ge(o_ready, c + 1)
                dve.sem_inc(mix_open, 1)
                assert at[0] == ML

        @block.tensor
        def _(pe):
            pe.wait_ge(consts, 9)
            for g in range(GR):
                pe.wait_ge(x0_ready, g + 1)
                for t in range(GB // CB):
                    for k in range(KT):
                        need(pe, x0_kept, (g * (GB // CB) + t) * KT + k - 1)
                        for b in range(CB):
                            ins = pe.transpose((f_bank, k_bank)[k][0:KP, b * S:(b + 1) * S],
                                               x0_g[g % 2][:, t * CB + b, k * KP:(k + 1) * KP], ident[:, :])
                        ins.then_inc(x0_turned, 1)

            def free_f(fi, use):
                if use == 0:
                    need(pe, dtu_ready, fi.count(IB, 0))
                elif use == 1:
                    pe.wait_ge(ln_ready, fi.count(1, 1))
                elif use < 5:
                    pe.wait_ge(tap_done, fi.count(IB * (KC - 1), (use - 1) * (KC - 1)))
                elif use < 8:
                    pe.wait_ge(z_ready, fi.count(IB, use - 4))
                elif use == 8:
                    pe.wait_ge(rest_ready, fi.count(1, 1))
                elif use < 12:
                    pe.wait_ge(rel_ready, fi.count(IB, use - 8))
                else:
                    pe.wait_ge(dtu_ready, fi.count(IB, use - 11))

            def norm_sum(fi, g=None):
                pe.wait_ge(sq_ready, fi.count(1, 1))
                free_f(fi, 0)
                if g is None:
                    pe.wait_ge(x0_kept, 2 * NCH)
                for k in range(KT):
                    ins = pe.matmul(f_bank[0:KP, :], onesm[:, :], xsq[:, k, :], start=(k == 0), stop=(k == KT - 1))
                ins.then_inc(f_full, 1)

            def in_proj(fi, m):
                if m == 0:
                    pe.wait_ge(wf_in, fi.layers(48))
                    pe.wait_ge(xn_ready, fi.count(1, 1))
                free_f(fi, 1 + m)
                for k in range(KT):
                    ins = pe.matmul(f_bank[:, :], w_in_v[:, k, m * 128:(m + 1) * 128], xn[:, k, :],
                                    start=(k == 0), stop=(k == KT - 1))
                ins.then_inc(f_full, 1)

            def x_proj(fi):
                pe.wait_ge(u_ready, fi.count(IB, IB))
                free_f(fi, 7)
                for k in range(IB):
                    ins = pe.matmul(f_bank[0:96, :], w_x_v[:, k, :], u_buf[:, fi.parity, k, :],
                                    start=(k == 0), stop=(k == IB - 1))
                ins.then_inc(f_full, 1)

            def dt_proj(fi, m):
                if m == 0:
                    pe.wait_ge(hi_ready, fi.count(2, 1))
                free_f(fi, 8 + m)
                pe.matmul(f_bank[:, :], wdt[:, m * 128:(m + 1) * 128], dtr[:, :], start=True, stop=True
                          ).then_inc(f_full, 1)

            def softplus_sum(fi, m):
                if m == 0:
                    pe.wait_ge(w1_ready, fi.count(1, 1))
                    pe.wait_ge(ln1_ready, fi.count(1, 1))
                free_f(fi, 11 + m)
                pe.matmul(f_bank[:, :], nident[:, :], dtu[:, fi.parity, m, :], start=True, stop=False)
                pe.matmul(f_bank[:, :], ident[:, :], exp_t[:, m, :], start=False, stop=False)
                pe.matmul(f_bank[:, :], ident[:, :], ndt[:, fi.parity, m, :], start=False, stop=False)
                pe.matmul(f_bank[:, :], ident[:, :], rel_t[:, m, :], start=False, stop=True).then_inc(f_full, 1)

            def spread_b(g, j):
                if j == 0:
                    pe.wait_ge(parts_ready, g.count(2, 2))
                    pe.wait_ge(hi_ready, g.count(2, 2))
                need(pe, scan_done, g.count(SLOTS, j - 1))
                for k in range(2):
                    n = 2 * (j % PAIRS) + k
                    ins = pe.matmul(b_bank[:, j % 2, k, :], sel[:, n, :], bc3[:, g.parity, :], start=True, stop=True)
                ins.then_inc(b_full, 1)

            def spread_c(g, n):
                if n == 0:
                    pe.wait_ge(parts_ready, g.count(2, 2))
                    pe.wait_ge(hi_ready, g.count(2, 2))
                need(pe, c_kept, g.count(NST, n))
                pe.matmul(c_bank[:, :], sel[:, NST + n, :], bc3[:, g.parity, :], start=True, stop=True
                          ).then_inc(c_full, 1)

            def sum_states(g, j):
                i, q = divmod(j, PAIRS)
                if q == 0:
                    need(pe, y_kept, g.count(IB, i))
                pe.wait_ge(cm_done, g.count(SLOTS, j + 1))
                for k in range(2):
                    for t in range(TILES):
                        ins = pe.matmul(y_bank[:, t * 128:(t + 1) * 128], state_c[:, j % 3, k, t * 128:(t + 1) * 128],
                                        ident[:, :], start=(q == 0 and k == 0 and t == 0),
                                        stop=(q == PAIRS - 1 and k == 1), is_transpose=True, skip_group_check=True)
                ins.then_inc(turned, 1)

            def y_back(g, i):
                pe.wait_ge(y_kept, g.count(IB, i + 1))
                if i == 0:
                    need(pe, x_ready, g.count(KT, 0))
                else:
                    pe.wait_ge(g_ready, g.count(IB, i))
                for t in range(TILES):
                    ins = pe.transpose(k_bank[:, t * 128:(t + 1) * 128], y_rows[:, t * 128:(t + 1) * 128], ident[:, :])
                ins.then_inc(k_full, 1)

            def out_proj(g, m):
                pe.wait_ge(gz_ready, g.count(IB, IB))
                if m == 1:
                    pe.wait_ge(x_ready, g.count(KT, 1))
                for k in range(IB):
                    ins = pe.matmul(k_bank[0:KP, :], w_out_v[:, k, m * KP:(m + 1) * KP], gated[:, k, :],
                                    start=(k == 0), stop=(k == IB - 1))
                ins.then_inc(k_full, 1)

            def step(g, first=False, front=True):
                f = g.plus(1)
                b = g.plus(-1)
                for j in range(SLOTS):
                    if j + 1 < SLOTS:
                        spread_b(g, j + 1)
                    elif front:
                        spread_b(f, 0)
                    if j < 2:
                        spread_c(g, 2 * (6 + j))
                    if j >= 18 and front:
                        spread_c(f, 2 * (j - 18))
                    if j >= 2:
                        sum_states(g, j - 2)
                    elif not first:
                        sum_states(b, SLOTS + j - 2)
                    if j < 2:
                        spread_c(g, 2 * (6 + j) + 1)
                    if j >= 18 and front:
                        spread_c(f, 2 * (j - 18) + 1)
                    if front and j == 1:
                        norm_sum(f, g)
                    if j == 2 and not first:
                        y_back(b, 2)
                    if j in (5, 6) and not first:
                        out_proj(b, j - 5)
                    if front and j in (4, 6, 8):
                        in_proj(f, (j - 4) // 2)
                    if j in (10, 18):
                        y_back(g, (j - 10) // 8)
                    if front and j in (10, 11, 12):
                        in_proj(f, j - 7)
                    if front and j == 13:
                        x_proj(f)
                    if front and j in (15, 16, 17):
                        dt_proj(f, j - 15)
                    if front and j in (20, 21, 22):
                        softplus_sum(f, j - 20)

            p = Step(0, 0)
            norm_sum(p)
            for m in range(6):
                in_proj(p, m)
            x_proj(p)
            for m in range(IB):
                dt_proj(p, m)
            for m in range(IB):
                softplus_sum(p, m)
            for n in range(12):
                spread_c(p, n)
            spread_b(p, 0)
            steps_loop(pe, step)
            last = Step(0, steps - 1)
            sum_states(last, SLOTS - 2)
            sum_states(last, SLOTS - 1)
            y_back(last, 2)
            out_proj(last, 0)
            out_proj(last, 1)

            pe.wait_ge(mw_in, 16 * 11)
            with pe.Fori(0, NCH) as c:
                pe.wait_ge(mix_open, c + 1)
                pe.wait_ge(xs_ready, c + 1)
                for t in range(TILES):
                    for k in range(KT):
                        ins = pe.transpose(xt_p[:, t // 2, t % 2, k * KP:(k + 1) * KP], xs[:, k, t * 128:(t + 1) * 128],
                                           ident[0:KP, 0:KP])
                ins.then_inc(xt_full, 1)
                pe.wait_ge(xf_ready, c + 1)
                for k in range(KT):
                    for t in range(TILES):
                        ins = pe.transpose(xft_p[:, k, t * 128:(t + 1) * 128], xf[:, t, k * KP:(k + 1) * KP], ident[:, :])
                ins.then_inc(xft_full, 1)
                pe.wait_ge(xft_ready, c + 1)
                for k in range(KT):
                    ins = pe.matmul(y_bank[:, :], p_v[:, k, :], xf_t[:, k, :], start=(k == 0), stop=(k == KT - 1))
                ins.then_inc(zt_full, 1)
                pe.wait_ge(zt_ready, c + 1)
                for t in range(TILES + 1):
                    if t < TILES:
                        if t >= 2:
                            pe.wait_ge(wt_ready, c * TILES + (t - 1))
                        pe.matmul(sc_p[t % 2][:, :], z_t[:, t * 128:(t + 1) * 128], cb_v, start=True, stop=True
                                  ).then_inc(sc_full, 1)
                    if t >= 1:
                        pe.wait_ge(wt_ready, c * TILES + t)
                        if t >= 2:
                            pe.wait_ge(wt_kept, c * TILES + (t - 1))
                        for sp in range(4):
                            ins = pe.transpose(c_bank[:, sp * 128:(sp + 1) * 128], wt[:, sp * 128:(sp + 1) * 128],
                                               ident[:, :])
                        ins.then_inc(wt_full, 1)
                pe.wait_ge(wt_kept, c * TILES + TILES)
                pe.wait_ge(wlo_ready, c + 1)
                for b in range(SP * NBLK + 2):
                    if b < SP * NBLK:
                        s, blk = divmod(b, NBLK)
                        sp, r = s // 2, 32 * (s // 2)
                        col = (s % 2) * ME * HD + blk * 128
                        if b >= 2:
                            pe.wait_ge(gelu_done, c * (SP * NBLK) + (b - 1))
                        pe.matmul(h1_p[:, b % 2, :], w1_v[r:r + 32, col:col + 128], z_t[r:r + 32, :],
                                  start=True, stop=True).then_inc(h1_full, 1)
                        if b >= 2:
                            pe.wait_ge(hg_ready, c * (SP * NBLK) + (b - 1))
                        for n in range(3):
                            ins = pe.matmul(gate_p[:, b % 2, :], gsel[:, (s % 2) * NBLK + blk, :], w_parts[n][:, sp, :],
                                            start=(n == 0), stop=(n == 2))
                        ins.then_inc(gate_full, 1)
                    if b >= 2:
                        d = b - 2
                        s, blk = divmod(d, NBLK)
                        sp, r = s // 2, 32 * (s // 2)
                        pe.wait_ge(hg_ready, c * (SP * NBLK) + (d + 1))
                        if d % (2 * NBLK) == 0:
                            pe.matmul(y_bank[r:r + 32, :], b2_v[:, sp, :], wt32[:, sp, :], start=True, stop=False)
                        last = d % (2 * NBLK) == 2 * NBLK - 1
                        ins = pe.matmul(y_bank[r:r + 32, :], w2_v[:, d, :], hid[:, 3 + d % 3, :], start=False, stop=last)
                        ins.then_inc(hg_used, 1)
                pe.wait_ge(comb_ready, c + 1)
                pe.matmul(f_bank[0:GH, :], g1_v, comb, start=True, stop=True).then_inc(g1_full, 1)
                pe.wait_ge(g1_ready, c + 1)
                for t in range(TILES):
                    ins = pe.matmul(xt_p[:, t // 2, t % 2, :], g1o[0:GH + 1, t * 128:(t + 1) * 128], g2_v,
                                    start=(t % 2 == 0), stop=True, skip_group_check=True)
                ins.then_inc(o_full, 1)


_INS = ['ids', 'type_ids', 'tok_w', 'pos_w', 'type_w', 'gamma', 'beta', 'w_in', 'w_front', 'w_dt', 'w_back', 'a_log',
        'final_w', 'p_w', 'c_blocks', 'w1', 'b1', 'w2', 'b2', 'g1', 'g1b', 'g2', 'g2b']


def lay_out(inputs):
    import numpy as np

    a = {k: np.asarray(v) for k, v in inputs.items()}
    m = {k[8:]: v for k, v in a.items() if k.startswith("L0_attn_")}
    f = {k[7:]: v for k, v in a.items() if k.startswith("L0_ffn_")}
    cat = np.concatenate

    def blocks(v):
        v = v.reshape(NL, IB, 128, -1)
        return v.transpose(0, 2, 1, 3).reshape(NL, 128, -1)

    x_proj = np.zeros((NL, 96, IN), np.float32)
    x_proj[:, :R] = m["x_proj_w"][:, :R]
    x_proj[:, 64:] = m["x_proj_w"][:, R:]
    in_t = m["in_proj_w"].transpose(0, 2, 1).reshape(NL, KT, KP, 2 * IN).transpose(0, 2, 1, 3).reshape(NL, KP, -1)
    w_in = cat([in_t, m["norm_w"].reshape(NL, KT, KP).transpose(0, 2, 1)], 2)
    w_front = cat([blocks(x_proj.transpose(0, 2, 1)), blocks(m["conv_w"]), blocks(m["conv_b"]),
                   blocks(m["dt_proj_b"])], 2)
    w_back = cat([blocks(m["out_proj_w"].transpose(0, 2, 1)), blocks(m["D"])], 2)
    c_blocks = np.zeros((SP, RR, SP, ME), np.float32)
    w1 = np.zeros((SP // 2, 2, RR, 2, ME, HD), np.float32)
    w2 = np.zeros((SP, NBLK, EB, HD, 2, RR), np.float32)
    b2 = np.zeros((SP // 2, 2, ME, 2, RR), np.float32)
    for s in range(SP):
        c_blocks[s, :, s] = f["C"][s].T
        w1[s // 2, s % 2, :, s % 2] = f["W1"][s].transpose(1, 0, 2)
        w2[s, :, :, :, s % 2] = f["W2"][s].reshape(NBLK, EB, HD, RR)
        b2[s // 2, s % 2, :, s % 2] = f["b2"][s]
    return {
        "ids": a["x"].T, "type_ids": a["mask_BS_i1_0"].T,
        "tok_w": a["L0_tok_tok_w"], "pos_w": a["L0_tok_pos_w"], "type_w": a["L0_tok_type_w"],
        "gamma": a["L0_tok_gamma"], "beta": a["L0_tok_beta"],
        "w_in": w_in, "w_front": w_front, "w_dt": m["dt_proj_w"].transpose(0, 2, 1), "w_back": w_back,
        "a_log": blocks(m["A_log"]), "final_w": m["final_norm_w"],
        "p_w": f["P"].transpose(1, 0, 2).reshape(KT, KP, SP * RR).transpose(1, 0, 2),
        "c_blocks": c_blocks.reshape(SP * RR, SP * ME),
        "w1": w1.reshape(SP * RR, 2 * ME * HD),
        "b1": f["b1"].reshape(SP * NBLK, EB * HD).T,
        "w2": w2.reshape(SP * NBLK, EB * HD, 2 * RR).transpose(1, 0, 2),
        "b2": b2.reshape(SP // 2, 2 * ME, 2 * RR).transpose(1, 0, 2),
        "g1": f["G1"], "g1b": f["g1b"].reshape(GH, 1),
        "g2": f["G2"], "g2b": f["g2b"],
    }


def kernel(**inputs):
    import numpy as np
    import concourse.bacc as bacc
    from concourse.bass_utils import run_bass_kernel_spmd

    nc = bacc.Bacc("TRN2", target_bir_lowering=False, num_devices=1)
    laid = lay_out(inputs)
    arrays, args = {}, []
    for name in _INS:
        v = np.ascontiguousarray(laid[name])
        arrays[f"in_{name}_dram"] = v
        args.append(nc.dram_tensor(f"in_{name}_dram", v.shape, mybir.dt.from_np(v.dtype), kind="ExternalInput").ap())
    h_scratch = nc.dram_tensor("h_scratch", (S, NB, H), F32, kind="Internal").ap()
    out = nc.dram_tensor("out_dram", (NB, S, H), F32, kind="ExternalOutput").ap()
    lm_tower(nc, *args, h_scratch, out)
    r = run_bass_kernel_spmd(nc, [arrays], core_ids=[0])
    return r.results[0]["out_dram"]
```

```python
from contextlib import ExitStack

import concourse.bass as bass
from concourse import mybir

F32 = mybir.dt.float32
BF16 = mybir.dt.bfloat16
I32 = mybir.dt.int32
ALU = mybir.AluOpType
ACT = mybir.ActivationFunctionType
AX = mybir.AxisListType

NB, S, H = 32, 128, 192
TOK = NB * S
KT, KP = 2, 96
NL, IN, NST, R, KC = 16, 384, 16, 48, 4
IB = IN // 128
CH = 512
CB = CH // S
NCH = TOK // CH
STEPS = NL * NCH
PAIRS = NST // 2
SLOTS = IB * PAIRS
EPS = 1e-5
SP, RR, ME, HD, GH = 8, 16, 64, 32, 64
TOPK = 4
TILES = CH // 128
EB = 4
NBLK = ME // EB


class Step:

    def __init__(self, it, s):
        self.it, self.s = it, s

    def plus(self, n):
        return Step(self.it, self.s + n)

    @property
    def parity(self):
        return self.s % 2

    def count(self, per, k):
        return self.it * (2 * per) + (self.s * per + k)

    def number(self):
        return self.it * 2 + self.s

    def tokens(self):
        return bass.ds((self.number() % NCH) * CH, CH)

    def layers(self, per):
        return (self.number() // NCH) * per + per


def need(eng, sem, value):
    if not isinstance(value, int) or value > 0:
        eng.wait_ge(sem, value)


def lm_tower(nc, ids, type_ids, tok_w, pos_w, type_w, gamma, beta, w_in, w_front, w_dt, w_back, a_log,
             final_w, p_w, c_blocks, w1, b1, w2, b2, g1, g1b, g2, g2b, h_scratch, out, steps=STEPS):
    ctx = ExitStack()
    with ctx:
        def sb(name, shape, dt=F32):
            return ctx.enter_context(nc.sbuf_tensor(name, shape, dt))

        def pb(name, shape):
            return ctx.enter_context(nc.psum_tensor(name, shape, F32))

        def sem(name):
            return ctx.enter_context(nc.semaphore(name))

        x_all = sb("x_all", [KP, KT, TOK])
        c_bc = sb("c_bc", [128, NST, CH])
        u_buf = sb("u_buf", [128, 2, IB, CH])
        z_buf = sb("z_buf", [128, 2, IB, CH])
        ndt = sb("ndt", [128, 2, IB, CH])
        dtu = sb("dtu", [128, 2, IB, CH])
        decay = sb("decay", [128, 3, 2, CB, S])
        state = sb("state", [128, 3, 2, CH])
        state_c = sb("state_c", [128, 3, 2, CH])
        exp_t = sb("exp_t", [128, IB, CH])
        rel_t = sb("rel_t", [128, IB, CH])
        xn = sb("xn", [KP, KT, CH])
        rs = sb("rs", [KP, CH])
        dtr = sb("dtr", [R, CH])
        bc3 = sb("bc3", [96, 2, CH], BF16)
        bc_mid = sb("bc_mid", [96, CH], BF16)
        bc_rest = sb("bc_rest", [96, CH])
        y_rows = sb("y_rows", [128, CH])
        gated = sb("gated", [128, IB, CH])
        sel = sb("sel", [96, 2 * NST, 128], BF16)
        ident = sb("ident", [128, 128])
        nident = sb("nident", [128, 128])
        win_x = sb("win", [128, KT * 2 * IN + KT])
        win = win_x[0:KP, :]
        wfr = sb("wfr", [128, IB * 96 + IB * (KC + 2)])
        wdt = sb("wdt", [R, IN])
        wbk = sb("wbk", [128, IB * H + IB])
        alog = sb("alog", [128, IB * NST])
        ea = sb("ea", [128, IB * NST])
        half = sb("half", [128, 1])
        epst = sb("epst", [128, 1])
        onesm = sb("onesm", [KP, KP])
        small = sb("small", [128, 6 * NB])

        w_in_v = win[:, 0:KT * 2 * IN].rearrange("p (k m) -> p k m", k=KT)
        nw_v = win[:, KT * 2 * IN:]
        w_x_v = wfr[:, 0:IB * 96].rearrange("p (k m) -> p k m", k=IB)
        o = IB * 96
        conv_w = wfr[:, o:o + IB * KC].rearrange("p (i k) -> p i k", i=IB)
        conv_b = wfr[:, o + IB * KC:o + IB * (KC + 1)]
        dt_b = wfr[:, o + IB * (KC + 1):o + IB * (KC + 2)]
        w_out_v = wbk[:, 0:IB * H].rearrange("p (k m) -> p k m", k=IB)
        d_v = wbk[:, IB * H:]

        b_bank = pb("b_bank", [128, 2, 2, CH])
        y_bank = pb("y_bank", [128, CH])
        c_bank = pb("c_bank", [128, CH])
        f_bank = pb("f_bank", [128, CH])
        k_bank = pb("k_bank", [128, CH])

        consts = sem("consts")
        dve_chain = sem("dve_chain")
        act_chain = sem("act_chain")
        pool_chain = sem("pool_chain")
        ids_in = sem("ids_in")
        tok_rows = [sem(f"tok_rows{i}") for i in range(4)]
        vec_in = sem("vec_in")
        centred = sem("centred")
        squared = sem("squared")
        var_ready = sem("var_ready")
        rstd_ready = sem("rstd_ready")
        h_ready = sem("h_ready")
        h_stored = sem("h_stored")
        x0_ready = sem("x0_ready")
        x0_turned = sem("x0_turned")
        x0_kept = sem("x0_kept")
        ww_in = sem("ww_in")
        wf_in = sem("wf_in")
        wa_in = sem("wa_in")
        wb_in = sem("wb_in")
        b_full = sem("b_full")
        decay_full = sem("decay_full")
        drive_ready = sem("drive_ready")
        scan_done = sem("scan_done")
        cm_done = sem("cm_done")
        turned = sem("turned")
        c_full = sem("c_full")
        c_kept = sem("c_kept")
        ea_ready = sem("ea_ready")
        sq_ready = sem("sq_ready")
        norm_full = sem("norm_full")
        f_full = sem("f_full")
        soft_full = sem("soft_full")
        ln_ready = sem("ln_ready")
        rs_ready = sem("rs_ready")
        xr_ready = sem("xr_ready")
        xn_ready = sem("xn_ready")
        c0_ready = sem("c0_ready")
        tap_done = sem("tap_done")
        thu_ready = sem("thu_ready")
        u_ready = sem("u_ready")
        thz_ready = sem("thz_ready")
        z_ready = sem("z_ready")
        hi_ready = sem("hi_ready")
        rest_ready = sem("rest_ready")
        mid_ready = sem("mid_ready")
        parts_ready = sem("parts_ready")
        abs_ready = sem("abs_ready")
        rel_ready = sem("rel_ready")
        exp_ready = sem("exp_ready")
        ln1_ready = sem("ln1_ready")
        w1_ready = sem("w1_ready")
        ndt_ready = sem("ndt_ready")
        dtu_ready = sem("dtu_ready")
        y_kept = sem("y_kept")
        k_full = sem("k_full")
        x_ready = sem("x_ready")
        g_ready = sem("g_ready")
        gz_ready = sem("gz_ready")
        mix_open = sem("mix_open")
        mw_in = sem("mw_in")
        h_back = sem("h_back")
        xs_ready = sem("xs_ready")
        xt_full = sem("xt_full")
        xsq_ready = sem("xsq_ready")
        xss_ready = sem("xss_ready")
        xln_ready = sem("xln_ready")
        xrs_ready = sem("xrs_ready")
        hc_ready = sem("hc_ready")
        hsq_ready = sem("hsq_ready")
        hvar_ready = sem("hvar_ready")
        hln_ready = sem("hln_ready")
        hrs_ready = sem("hrs_ready")
        xf_ready = sem("xf_ready")
        xft_full = sem("xft_full")
        xft_ready = sem("xft_ready")
        zt_full = sem("zt_full")
        zt_ready = sem("zt_ready")
        sc_full = sem("sc_full")
        dif_ready = sem("dif_ready")
        exs_ready = sem("exs_ready")
        wt_ready = sem("wt_ready")
        wt_full = sem("wt_full")
        wt_kept = sem("wt_kept")
        whi_ready = sem("whi_ready")
        wrest_ready = sem("wrest_ready")
        wmid_ready = sem("wmid_ready")
        wlo_ready = sem("wlo_ready")
        g_in = [sem(f"g_in{i}") for i in range(2)]
        w1_full = sem("w1_full")
        w1_hi_ready = sem("w1_hi_ready")
        w1_rest_ready = sem("w1_rest_ready")
        w1_mid_ready = sem("w1_mid_ready")
        w1_built = sem("w1_built")
        zs_full = sem("zs_full")
        zhi_ready = sem("zhi_ready")
        zrest_ready = sem("zrest_ready")
        zmid_ready = sem("zmid_ready")
        z_built = sem("z_built")
        h1_full = sem("h1_full")
        gelu_done = sem("gelu_done")
        gate_full = sem("gate_full")
        hg_ready = sem("hg_ready")
        hg_used = sem("hg_used")
        comb_ready = sem("comb_ready")
        g1_full = sem("g1_full")
        g1_ready = sem("g1_ready")
        o_full = sem("o_full")
        o_ready = sem("o_ready")
        mchain = sem("mchain")
        out_done = sem("out_done")
        stored = sem("stored")

        PROD_BANKS = (f_bank, k_bank, f_bank, k_bank, f_bank, c_bank, k_bank, f_bank, c_bank, k_bank,
                      f_bank, k_bank, c_bank)
        XP, DT, SOFT = 2 * IB, 2 * IB + 1, 3 * IB + 1
        FUSES = SOFT
        BACK_BANKS = (k_bank, k_bank, c_bank, c_bank, c_bank)
        KUSES = len(BACK_BANKS)
        C_SLOT = 20
        C_EARLY = SLOTS - C_SLOT

        block = ctx.enter_context(nc.Block())

        def steps_loop(eng, step):
            step(Step(0, 0), first=True)
            step(Step(0, 1))
            if steps > 4:
                with eng.Fori(1, steps // 2 - 1) as it:
                    step(Step(it, 0))
                    step(Step(it, 1))
            step(Step(0, steps - 2), norm=False)
            step(Step(0, steps - 1), norm=False, front=False)

        GR = 4
        GB = NB // GR
        emb = c_bc[:, :, :].rearrange("p a b -> p (a b)")[:, 0:NB * H].rearrange("p (b h) -> p b h", b=NB)
        typ = u_buf[:, :, :, :].rearrange("p a i t -> p (a i t)")
        typ2 = z_buf[:, :, :, :].rearrange("p a i t -> p (a i t)")
        typ_g = [(typ, typ2)[g // 2][:, (g % 2) * GB * H:(g % 2 + 1) * GB * H].rearrange(
            "p (b h) -> p b h", b=GB) for g in range(GR)]
        sq_g = ndt[:, :, :, :].rearrange("p a i t -> p (a i t)")[:, 0:GB * H].rearrange("p (b h) -> p b h", b=GB)
        x0_g = [dtu[:, :, :, :].rearrange("p a i t -> p (a i t)")[:, g * GB * H:(g + 1) * GB * H].rearrange(
            "p (b h) -> p b h", b=GB) for g in range(2)]
        vecs = exp_t[:, :, :].rearrange("p a b -> p (a b)")
        pos_v, gam_v, bet_v = (vecs[:, i * H:(i + 1) * H] for i in range(3))
        id_v = y_rows[:, 0:2 * NB].bitcast(I32)
        st_sum, st_mean, st_var, st_ln, st_rstd = (small[:, i * GB:(i + 1) * GB] for i in range(5))

        def flat(t):
            return t.rearrange("p a i t -> p (a i t)")

        def exp_flat(t):
            return t[:, :, :].rearrange("p i t -> p (i t)")

        uf, zf, nf, df = (flat(t[:, :, :, :]) for t in (u_buf, z_buf, ndt, dtu))
        sf, scf = flat(state[:, :, :, :]), flat(state_c[:, :, :, :])
        dcf = decay[:, :, :, :, :].rearrange("p r a b t -> p (r a b t)")
        cf = c_bc[:, :, :].rearrange("p a b -> p (a b)")
        NW1 = ME * HD
        rf, gf = exp_flat(rel_t), exp_flat(gated)
        w1_s = cf.bitcast(BF16).rearrange("p (s m) -> p s m", s=SP)
        z_s = nf[:, 5 * CH:6 * CH].bitcast(BF16).rearrange("p (r t) -> p r t", r=2)
        selz = gf[:, CH:3 * CH].rearrange("p (s g r) -> p s g r", s=SP, g=8)
        z_hi, z_mid = (y_rows[:, i * (CH // 2):(i + 1) * (CH // 2)].bitcast(BF16) for i in range(2))
        z_rest = win_x[:, 2 * CH:3 * CH]
        w1_c, w1_rest = dcf[:, 0:NW1], zf[:, 0:NW1]
        w1_hi, w1_mid = (t[:, 2 * 1024:3 * 1024].bitcast(BF16) for t in (dcf, sf))
        mid_z, low_z, mid_w, low_w, mid_w2 = (small[:, i:i + 1] for i in range(177, 182))
        w2_v = [t[:, 0:2048].rearrange("p (b m) -> p b m", m=2 * RR) for t in (uf, df)]
        g_parts = sel[:, :, :].rearrange("p n m -> p (n m)").rearrange("p (r q t) -> p r q t", r=2, q=4)
        gsel = df[0:96, 2048:2560].bitcast(BF16).rearrange("p (b m) -> p b m", m=128)
        id_sum = y_rows[0:96, 0:32]
        cb_v = uf[:, 2048:2560]
        p_v = uf[0:KP, 2560:2816].rearrange("p (k m) -> p k m", k=KT)
        b1_v = uf[:, 2816:2944]
        b2_v = uf[:, 2944:3072].rearrange("p (s m) -> p s m", m=2 * RR)
        g1_v, g1b_v = wfr[:, 0:GH], wfr[0:GH, GH:GH + 1]
        fw_v, g2_v = wbk[:, 0:H], wbk[0:GH + 1, H:2 * H]

        def tiles(v):
            return v.rearrange("p (t h) -> p t h", t=TILES)

        h_in, h2, xf, sqm = (tiles(zf[:, i * TILES * H:(i + 1) * TILES * H]) for i in range(4))
        xs = exp_t[0:KP, 0:KT, :]
        xf_t = nf[0:KP, 0:KT * CH].rearrange("p (k t) -> p k t", k=KT)
        z_t, comb, g1o = (nf[:, i * CH:(i + 1) * CH] for i in (2, 3, 4))
        rep, dif, exs = (rf[:, i * CH:(i + 1) * CH] for i in range(3))
        wt = gf[:, 0:CH]
        wt32 = sf[:, 0:4 * CH].rearrange("p (s t) -> p s t", s=4)
        wrest = dcf[:, 0:4 * CH].rearrange("p (s t) -> p s t", s=4)
        w_parts = [cfx.bitcast(BF16).rearrange("p (s t) -> p s t", s=4)
                   for cfx in (dcf[:, 2048:3072], sf[:, 2048:3072], win_x[:, 0:1024])]
        W_LOADS = 12
        b_all = b_bank[:, :, :, :].rearrange("p a b t -> p (a b t)")

        def selz_of(s):
            return selz[:, s, :, :].rearrange("p g r -> p (g r)")

        def zs_bank(s):
            return gate_p[:, 0, :] if s == 0 else f_bank[:, :]

        hid = scf.rearrange("p (r t) -> p r t", t=CH)
        sm_ss, sm_ln, sm_rs, sm_sum, sm_mean, sm_var, sm_vln, sm_rstd = (small[:, 4 * i:4 * i + 4] for i in range(8))
        top8 = small[:, 32:96].rearrange("p (s k) -> p s k", s=SP)
        top4 = small[:, 96:160].rearrange("p (s k) -> p s k", s=SP)
        den, rden = small[:, 160:168], small[:, 168:176]
        xt_p = b_bank[:, 0, :, 0:2 * H].rearrange("p a (b h) -> p a b h", b=2)
        xft_p = b_bank[0:KP, 1, :, :]
        sc_p = (f_bank, k_bank)
        h1_p, gate_p = (b_bank[:, i, :, :] for i in range(2))
        LOW = -3.0e38

        @block.sync
        def _(sp):
            sp.dma_start(id_v[:, 0:NB], ids).then_inc(ids_in, 16)
            sp.dma_start(id_v[:, NB:2 * NB], type_ids).then_inc(ids_in, 16)
            sp.dma_start(pos_v, pos_w).then_inc(vec_in, 16)
            sp.dma_start(gam_v, gamma.partition_broadcast(128)).then_inc(vec_in, 16)
            sp.dma_start(bet_v, beta.partition_broadcast(128)).then_inc(vec_in, 16)

            def load_layer(layer):
                first = layer * NCH
                later = not isinstance(first, int) or first > 0
                if later:
                    sp.wait_ge(z_ready, first * IB)
                sp.dma_start(win[:, :], w_in[bass.ds(layer, 1)].rearrange("a p m -> (a p) m")).then_inc(ww_in, 16)
                if later:
                    sp.wait_ge(rel_ready, first * IB)
                sp.dma_start(wfr[:, :], w_front[bass.ds(layer, 1)].rearrange("a p m -> (a p) m")).then_inc(wf_in, 16)
                sp.dma_start(wdt[:, :], w_dt[bass.ds(layer, 1)].rearrange("a p m -> (a p) m")).then_inc(wf_in, 16)
                if later:
                    sp.wait_ge(ea_ready, first)
                sp.dma_start(alog[:, :], a_log[bass.ds(layer, 1)].rearrange("a p m -> (a p) m")).then_inc(wa_in, 16)
                if later:
                    sp.wait_ge(x_ready, first * KT)
                sp.dma_start(wbk[:, :], w_back[bass.ds(layer, 1)].rearrange("a p m -> (a p) m")).then_inc(wb_in, 16)

            nl = (steps + NCH - 1) // NCH
            load_layer(0)
            for g in range(GR):
                sp.wait_ge(h_ready, g + 1)
                sp.dma_start(h_scratch[:, g * GB:(g + 1) * GB, :], emb[:, g * GB:(g + 1) * GB, :]).then_inc(h_stored, 16)
            if nl > 1:
                with sp.Fori(1, nl) as layer:
                    load_layer(layer)
            sp.wait_ge(h_stored, 16 * GR)

            sp.wait_ge(mix_open, 1)
            for dst, src in ((w1_c, w1), (w2_v[0], w2[:, 0:64, :]), (w2_v[1], w2[:, 64:128, :]), (cb_v, c_blocks), (p_v, p_w), (b1_v, b1), (b2_v, b2),
                             (g1_v, g1), (g1b_v, g1b), (fw_v, final_w.partition_broadcast(128)),
                             (g2_v[0:GH, :], g2), (g2_v[GH:GH + 1, :], g2b.rearrange("(a h) -> a h", a=1))):
                sp.dma_start(dst, src).then_inc(mw_in, 16)
            sp.wait_ge(w1_built, SP)
            with sp.Fori(0, NCH) as c:
                sp.wait_ge(mix_open, c + 1)
                sp.dma_start(h_in, h_scratch[:, bass.ds(c * CB, CB), :]).then_inc(h_back, 16)
                sp.wait_ge(wlo_ready, c + 1)
                for pair in range(4):
                    if pair >= 2:
                        sp.wait_ge(gate_full, c * (SP * NBLK) + 2 * NBLK * (pair - 1))
                    for n in range(3):
                        for q in range(4):
                            sp.dma_start(g_parts[32 * n:32 * n + 32, pair % 2, q, :],
                                         w_parts[n][32 * q:32 * q + 32, pair, :]).then_inc(g_in[pair % 2], 16)
                sp.wait_ge(o_ready, c + 1)
                sp.dma_start(out[bass.ds(c * CB, CB), :, :].rearrange("b s h -> s b h"), xf).then_inc(out_done, 16)
                sp.wait_ge(out_done, c * 16 + 16)
                sp.sem_inc(stored, 1)


        @block.gpsimd
        def _(pool):
            pool.memset(ident[:, :], 0.0).then_inc(pool_chain, 1)
            pool.memset(nident[:, :], 0.0).then_inc(pool_chain, 1)
            pool.memset(sel[:, :, :], 0.0).then_inc(pool_chain, 1)
            pool.memset(half[:, :], 0.5).then_inc(pool_chain, 1)
            pool.memset(epst[:, :], EPS).then_inc(consts, 1)
            pool.memset(onesm[:, :], 1.0).then_inc(consts, 1)
            pool.memset(decay[:, :, :, :, 0:1], 0.0).then_inc(consts, 1)
            pool.wait_ge(pool_chain, 4)
            for m, fill in ((ident, 1.0), (nident, -1.0)):
                pool.affine_select(out=m[:, :], in_=m[:, :], compare_op=ALU.not_equal, fill=fill, base=0,
                                   pattern=[[-1, 128]], channel_multiplier=1).then_inc(consts, 1)
            pool.wait_ge(consts, 5)
            pool.memset(half[64:64 + NST, :], 0.25).then_inc(consts, 1)
            for part in range(3):
                pool.wait_ge(consts, 6 + part)
                pool.affine_select(out=sel[32 * part:32 * part + 32, :, :], in_=sel[32 * part:32 * part + 32, :, :],
                                   compare_op=ALU.not_equal, fill=1.0, base=0,
                                   pattern=[[-1, 2 * NST], [0, 128]], channel_multiplier=1).then_inc(consts, 1)
            pool.wait_ge(consts, 9)
            pool.wait_ge(ids_in, 32)
            for b in range(NB):
                g = b // GB
                pool.indirect_dma_start(emb[:, b, :], None, tok_w, bass.IndirectOffsetOnAxis(id_v[:, b:b + 1], 0)
                                        ).then_inc(tok_rows[g], 16)
                pool.indirect_dma_start(typ_g[g][:, b % GB, :], None, type_w,
                                        bass.IndirectOffsetOnAxis(id_v[:, NB + b:NB + b + 1], 0)
                                        ).then_inc(tok_rows[g], 16)

            def scale_x(fi):
                pool.wait_ge(rs_ready, fi.count(1, 1))
                pool.wait_ge(xr_ready, fi.count(1, 1))
                pool.tensor_tensor(xn[:, :, :], xn[:, :, :], rs[:, :].unsqueeze(1).to_broadcast([KP, KT, CH]), ALU.mult
                                   ).then_inc(xn_ready, 1)

            def times_c(g, j):
                pool.wait_ge(scan_done, g.count(SLOTS, j + 1))
                if j < PAIRS:
                    pool.wait_ge(c_kept, g.count(NST, 2 * j + 2))
                need(pool, turned, g.count(SLOTS, j - 2))
                q = j % PAIRS
                pool.tensor_tensor(state_c[:, j % 3, :, :], state[:, j % 3, :, :], c_bc[:, 2 * q:2 * q + 2, :],
                                   ALU.mult).then_inc(cm_done, 1)

            def gate_z(g, i):
                pool.wait_ge(g_ready, g.count(IB, i + 1))
                if i == 0:
                    pool.wait_ge(z_ready, g.count(IB, IB))
                pool.tensor_tensor(gated[:, i, :], gated[:, i, :], z_buf[:, g.parity, i, :], ALU.mult
                                   ).then_inc(gz_ready, 1)

            def take_dtu(fi, m):
                pool.wait_ge(ndt_ready, fi.count(IB, m + 1))
                pool.tensor_tensor(dtu[:, fi.parity, m, :], u_buf[:, fi.parity, m, :], ndt[:, fi.parity, m, :], ALU.mult
                                   ).then_inc(dtu_ready, 1)

            def step(g, first=False, front=True, norm=True):
                for j in range(SLOTS):
                    times_c(g, j)
                    if j == 1:
                        take_dtu(g, 1)
                    if j == 8:
                        take_dtu(g, 2)
                    if j == 21 and front:
                        take_dtu(g.plus(1), 0)
                    if j == 5 and not first:
                        gate_z(g.plus(-1), 2)
                    if j in (12, 20):
                        gate_z(g, (j - 12) // 8)
                    if norm and j == 22:
                        scale_x(g.plus(2))

            scale_x(Step(0, 0))
            scale_x(Step(0, 1))
            take_dtu(Step(0, 0), 0)
            steps_loop(pool, step)
            gate_z(Step(0, steps - 1), 2)

        @block.scalar
        def _(act):
            act.wait_ge(consts, 9)
            for g in range(GR):
                for half_ln in range(2):
                    k = 2 * g + half_ln
                    act.wait_ge(centred, k + 1)
                    act.activation(sq_g, (emb[:, g * GB:(g + 1) * GB, :], x0_g[g % 2])[half_ln], ACT.Square
                                   ).then_inc(squared, 1)
                    act.wait_ge(var_ready, k + 1)
                    act.activation(st_ln, st_var, ACT.Ln, bias=epst[:, 0:1], scale=1.0 / H).then_inc(act_chain, 1)
                    act.wait_ge(act_chain, k + 1)
                    act.activation(st_rstd, st_ln, ACT.Exp, scale=-0.5).then_inc(rstd_ready, 1)
                for t in range(GB // CB):
                    for k in range(KT):
                        n = (g * (GB // CB) + t) * KT + k
                        act.wait_ge(x0_turned, n + 1)
                        c = g * (GB // CB) + t
                        act.activation(x_all[:, k, c * CH:(c + 1) * CH], (f_bank, k_bank)[k][0:KP, :], ACT.Copy
                                       ).then_inc(x0_kept, 1)

            def square(fi):
                need(act, x_ready, fi.count(KT, -3 * KT))
                need(act, f_full, fi.count(FUSES, 2 * IB - FUSES))
                act.activation(xn[:, :, :], x_all[:, :, fi.tokens()], ACT.Square).then_inc(sq_ready, 1)

            def ln_square(fi):
                act.wait_ge(norm_full, fi.count(1, 1))
                need(act, xn_ready, fi.count(1, 0))
                act.activation(rs[:, :], f_bank[0:KP, :], ACT.Ln, bias=epst[0:KP, 0:1], scale=1.0 / H
                               ).then_inc(ln_ready, 1)

            def inverse_rms(fi):
                act.wait_ge(ln_ready, fi.count(1, 1))
                act.wait_ge(ww_in, fi.layers(16))
                act.activation(rs[:, :], rs[:, :], ACT.Exp, scale=-0.5).then_inc(rs_ready, 1)

            def weigh_x(fi):
                for k in range(KT):
                    ins = act.activation(xn[:, k, :], x_all[:, k, fi.tokens()], ACT.Copy, scale=nw_v[:, k:k + 1])
                ins.then_inc(xr_ready, 1)

            def conv_first(fi, m):
                if m == 0:
                    act.wait_ge(wf_in, fi.layers(32))
                act.wait_ge(f_full, fi.count(FUSES, 1 + m))
                need(act, g_ready, fi.count(IB, m + 1 - 2 * IB))
                act.activation(u_buf[:, fi.parity, m, :], PROD_BANKS[m][:, :], ACT.Identity,
                               scale=conv_w[:, m, KC - 1:KC], bias=conv_b[:, m:m + 1]).then_inc(c0_ready, 1)

            def tanh_u(fi, m):
                act.wait_ge(tap_done, fi.count(IB * (KC - 1), (m + 1) * (KC - 1)))
                act.activation(exp_t[:, m, :], u_buf[:, fi.parity, m, :], ACT.Tanh, scale=0.5).then_inc(thu_ready, 1)

            def tanh_z(fi, m):
                act.wait_ge(f_full, fi.count(FUSES, IB + m + 1))
                need(act, gz_ready, fi.count(IB, m + 1 - 2 * IB))
                act.activation(z_buf[:, fi.parity, m, :], PROD_BANKS[IB + m][:, :], ACT.Tanh, scale=0.5
                               ).then_inc(thz_ready, 1)

            def take_x_proj(fi):
                act.wait_ge(f_full, fi.count(FUSES, XP + 1))
                act.activation(dtr[:, :], PROD_BANKS[XP][0:R, :], ACT.Copy, scale=0.5).then_inc(hi_ready, 1)
                act.activation(bc3[64:96, fi.parity, :], PROD_BANKS[XP][64:96, :], ACT.Copy, scale=half[64:96, 0:1]
                               ).then_inc(hi_ready, 1)

            def middle(fi):
                act.wait_ge(rest_ready, fi.count(1, 1))
                act.activation(bc_mid[64:96, :], bc_rest[64:96, :], ACT.Copy).then_inc(mid_ready, 1)
                act.wait_ge(mid_ready, fi.count(1, 1))
                act.activation(bc3[32:64, fi.parity, :], bc_mid[64:96, :], ACT.Copy).then_inc(parts_ready, 1)

            def abs_relu(fi, m):
                act.wait_ge(f_full, fi.count(FUSES, DT + m + 1))
                act.wait_ge(u_ready, fi.count(IB, IB))
                x = PROD_BANKS[DT + m][:, :]
                act.activation(exp_t[:, m, :], x, ACT.Abs, bias=dt_b[:, m:m + 1]).then_inc(abs_ready, 1)
                act.activation(rel_t[:, m, :], x, ACT.Relu, bias=dt_b[:, m:m + 1]).then_inc(rel_ready, 1)

            def soft_exp(fi):
                act.wait_ge(abs_ready, fi.count(IB, IB))
                act.activation(exp_t[:, :, :], exp_t[:, :, :], ACT.Exp, scale=-1.0).then_inc(exp_ready, 1)

            def soft_ln(fi):
                act.wait_ge(exp_ready, fi.count(1, 1))
                act.activation(ndt[:, fi.parity, :, :], exp_t[:, :, :], ACT.Ln, bias=1.0).then_inc(ln1_ready, 1)

            def take_ndt(fi, m):
                act.wait_ge(soft_full, fi.count(IB, m + 1))
                act.activation(ndt[:, fi.parity, m, :], PROD_BANKS[SOFT + m][:, :], ACT.Copy, scale=-1.0
                               ).then_inc(ndt_ready, 1)

            def take_a(fi):
                act.wait_ge(wa_in, fi.layers(16))
                need(act, decay_full, fi.count(2 * SLOTS, 0))
                act.activation(ea[:, :], alog[:, :], ACT.Exp).then_inc(ea_ready, 1)

            def decays(g, j):
                i, q = divmod(j, PAIRS)
                if j % PAIRS == 0:
                    act.wait_ge(ndt_ready, g.count(IB, i + 1))
                if j == 0:
                    act.wait_ge(ea_ready, g.count(1, 1))
                need(act, scan_done, g.count(SLOTS, j - 2))
                nd = ndt[:, g.parity, i, :].rearrange("p (b t) -> p b t", b=CB)
                for k in range(2):
                    n = i * NST + 2 * q + k
                    act.activation(decay[:, j % 3, k, :, 1:S], nd[:, :, 1:S], ACT.Exp, scale=ea[:, n:n + 1]
                                   ).then_inc(decay_full, 1)

            def keep_c(g, n):
                act.wait_ge(c_full, g.count(NST, n + 1))
                if n % 2 == 0:
                    need(act, cm_done, g.count(SLOTS, n // 2 + 1 - PAIRS))
                act.activation(c_bc[:, n, :], c_bank[:, :], ACT.Copy).then_inc(c_kept, 1)

            def keep_y(g, i):
                act.wait_ge(turned, g.count(SLOTS, PAIRS * (i + 1)))
                need(act, k_full, g.count(KUSES, i - (2 if i == 0 else 0)))
                act.activation(y_rows[:, :], y_bank[:, :], ACT.Copy, scale=-2.0).then_inc(y_kept, 1)

            def step(g, first=False, front=True, norm=True):
                f, h = g.plus(1), g.plus(2)
                for j in range(SLOTS):
                    if j <= PAIRS - C_EARLY:
                        keep_c(g, 2 * (j + C_EARLY - 1) + 1)
                    if j > C_SLOT and front:
                        keep_c(f, 2 * (j - C_SLOT - 1) + 1)
                    if j + 2 < SLOTS:
                        decays(g, j + 2)
                    elif front:
                        decays(f, j + 2 - SLOTS)
                    if j < PAIRS - C_EARLY:
                        keep_c(g, 2 * (j + C_EARLY))
                    if j >= C_SLOT and front:
                        keep_c(f, 2 * (j - C_SLOT))
                    if j == 0:
                        take_ndt(g, 1)
                    if j in (1, 3) and front:
                        conv_first(f, j // 2)
                    if j == 2 and not first:
                        keep_y(g.plus(-1), 2)
                    if j in (10, 18):
                        keep_y(g, (j - 10) // 8)
                    if j == 8:
                        take_ndt(g, 2)
                    if front:
                        if j == 6:
                            conv_first(f, 2)
                        if j in (5, 8, 11):
                            tanh_u(f, (j - 5) // 3)
                        if j in (9, 12, 13):
                            tanh_z(f, (9, 12, 13).index(j))
                        if j == 14:
                            take_x_proj(f)
                        if j == 15:
                            middle(f)
                        if j == 16:
                            abs_relu(f, 0)
                            abs_relu(f, 1)
                        if j == 17:
                            abs_relu(f, 2)
                            soft_exp(f)
                    if norm and j == 13:
                        square(h)
                    if norm and j == 18:
                        ln_square(h)
                    if front and j == 18:
                        soft_ln(f)
                    if norm and j == 21:
                        inverse_rms(h)
                    if front:
                        if j == 21:
                            take_ndt(f, 0)
                            take_a(f)
                    if norm and j == 22:
                        weigh_x(h)

            p = Step(0, 0)
            act.wait_ge(x0_kept, 2 * NCH)
            square(p)
            ln_square(p)
            inverse_rms(p)
            weigh_x(p)
            for m in range(IB):
                conv_first(p, m)
                tanh_u(p, m)
            for m in range(IB):
                tanh_z(p, m)
            square(p.plus(1))
            take_x_proj(p)
            middle(p)
            for m in range(IB):
                abs_relu(p, m)
            soft_exp(p)
            ln_square(p.plus(1))
            soft_ln(p)
            inverse_rms(p.plus(1))
            weigh_x(p.plus(1))
            take_a(p)
            take_ndt(p, 0)
            act.wait_ge(h_stored, 16 * GR)
            for n in range(2 * C_EARLY - 1):
                keep_c(p, n)
            decays(p, 0)
            decays(p, 1)
            steps_loop(act, step)
            keep_y(Step(0, steps - 1), 2)

            for s in range(SP):
                act.wait_ge(w1_full, s + 1)
                if s > 0:
                    act.wait_ge(w1_rest_ready, s)
                act.activation(w1_hi, b_all, ACT.Copy).then_inc(w1_hi_ready, 1)
                act.wait_ge(w1_rest_ready, s + 1)
                if s > 0:
                    act.wait_ge(w1_built, s)
                act.activation(w1_mid, w1_rest, ACT.Copy).then_inc(w1_mid_ready, 1)

            def z_high(c, s):
                act.wait_ge(zs_full, c * SP + (s + 1))
                if s > 0:
                    act.wait_ge(zrest_ready, c * SP + s)
                act.activation(z_hi, zs_bank(s), ACT.Copy).then_inc(zhi_ready, 1)

            def z_middle(c, s):
                act.wait_ge(zrest_ready, c * SP + (s + 1))
                if s > 0:
                    act.wait_ge(z_built, c * SP + s)
                act.activation(z_mid, z_rest, ACT.Copy).then_inc(zmid_ready, 1)

            with act.Fori(0, NCH) as c:
                act.wait_ge(mix_open, c + 1)
                act.activation(xs, x_all[:, :, bass.ds(c * CH, CH)], ACT.Copy).then_inc(xs_ready, 1)
                act.wait_ge(xt_full, c + 1)
                act.activation(sqm.rearrange("p (a b) h -> p a b h", a=2), xt_p, ACT.Square).then_inc(xsq_ready, 1)
                act.wait_ge(xss_ready, c + 1)
                act.activation(sm_ln, sm_ss, ACT.Ln, bias=epst[:, 0:1], scale=1.0 / H).then_inc(xln_ready, 1)
                act.wait_ge(xln_ready, c + 1)
                act.activation(sm_rs, sm_ln, ACT.Exp, scale=-0.5).then_inc(xrs_ready, 1)
                act.wait_ge(hc_ready, c + 1)
                act.activation(sqm, xf, ACT.Square).then_inc(hsq_ready, 1)
                act.wait_ge(hvar_ready, c + 1)
                act.activation(sm_vln, sm_var, ACT.Ln, bias=epst[:, 0:1], scale=1.0 / H).then_inc(hln_ready, 1)
                act.wait_ge(hln_ready, c + 1)
                act.activation(sm_rstd, sm_vln, ACT.Exp, scale=-0.5).then_inc(hrs_ready, 1)
                act.wait_ge(xft_full, c + 1)
                act.activation(xf_t, xft_p, ACT.Copy).then_inc(xft_ready, 1)
                act.wait_ge(zt_full, c + 1)
                act.activation(z_t, y_bank[:, :], ACT.Copy).then_inc(zt_ready, 1)
                z_high(c, 0)
                z_middle(c, 0)
                for t in range(TILES):
                    act.wait_ge(dif_ready, c * TILES + (t + 1))
                    act.activation(exs, dif, ACT.Exp).then_inc(exs_ready, 1)
                    act.wait_ge(wt_full, c * TILES + (t + 1))
                    act.activation(wt32[:, :, t * 128:(t + 1) * 128],
                                   c_bank[:, :].rearrange("p (s t) -> p s t", s=4), ACT.Copy).then_inc(wt_kept, 1)
                act.wait_ge(wt_kept, c * TILES + TILES)
                act.activation(w_parts[0], wt32, ACT.Copy).then_inc(whi_ready, 1)
                act.wait_ge(wrest_ready, c + 1)
                act.activation(w_parts[1], wrest, ACT.Copy).then_inc(wmid_ready, 1)
                for b in range(SP * NBLK):
                    act.wait_ge(h1_full, c * (SP * NBLK) + (b + 1))
                    if b >= 3:
                        act.wait_ge(hg_ready, c * (SP * NBLK) + (b - 2))
                    act.activation(hid[:, b % 3, :], h1_p[:, b % 2, :], ACT.Gelu_apprx_tanh, bias=b1_v[:, b:b + 1]
                                   ).then_inc(gelu_done, 1)
                    if b % NBLK == 4 and b // NBLK + 1 < SP:
                        z_high(c, b // NBLK + 1)
                    if b % NBLK == 7 and b // NBLK + 1 < SP:
                        z_middle(c, b // NBLK + 1)
                act.wait_ge(hg_used, c * (SP * NBLK) + SP * NBLK)
                act.activation(comb, y_bank[:, :], ACT.Copy).then_inc(comb_ready, 1)
                act.wait_ge(g1_full, c + 1)
                act.activation(g1o[0:GH, :], f_bank[0:GH, :], ACT.Gelu_apprx_tanh, bias=g1b_v).then_inc(g1_ready, 1)

        @block.vector
        def _(dve):
            chain = [0]

            def link(ins):
                chain[0] += 1
                ins.then_inc(dve_chain, 1)
                dve.wait_ge(dve_chain, chain[0])

            def layer_norm(src, dst, k):
                link(dve.tensor_reduce(st_sum, src, AX.X, ALU.add))
                link(dve.tensor_scalar(st_mean, st_sum, 1.0 / H, None, ALU.mult))
                dve.tensor_tensor(dst, src, st_mean.unsqueeze(2).to_broadcast([128, GB, H]), ALU.subtract
                                  ).then_inc(centred, 1)
                dve.wait_ge(squared, k + 1)
                dve.tensor_reduce(st_var, sq_g, AX.X, ALU.add).then_inc(var_ready, 1)
                dve.wait_ge(rstd_ready, k + 1)
                return dve.tensor_tensor(dst, dst, st_rstd.unsqueeze(2).to_broadcast([128, GB, H]), ALU.mult)

            dve.wait_ge(vec_in, 48)
            for g in range(GR):
                e = emb[:, g * GB:(g + 1) * GB, :]
                dve.wait_ge(tok_rows[g], 32 * GB)
                link(dve.tensor_tensor(e, e, pos_v.unsqueeze(1).to_broadcast([128, GB, H]), ALU.add))
                link(dve.tensor_tensor(e, e, typ_g[g], ALU.add))
                link(layer_norm(e, e, 2 * g))
                link(dve.tensor_tensor(e, e, gam_v.unsqueeze(1).to_broadcast([128, GB, H]), ALU.mult))
                link2 = dve.tensor_tensor(e, e, bet_v.unsqueeze(1).to_broadcast([128, GB, H]), ALU.add)
                link2.then_inc(h_ready, 1)
                dve.wait_ge(h_ready, g + 1)
                if g >= 2:
                    dve.wait_ge(x0_turned, (g - 1) * (GB // CB) * KT)
                layer_norm(e, x0_g[g % 2], 2 * g + 1).then_inc(x0_ready, 1)

            def tap(fi, m, k):
                u = u_buf[:, fi.parity, m, :].rearrange("p (b t) -> p b t", b=CB)
                f = PROD_BANKS[m][:, :].rearrange("p (b t) -> p b t", b=CB)
                if k == 1:
                    dve.wait_ge(c0_ready, fi.count(IB, m + 1))
                else:
                    dve.wait_ge(tap_done, fi.count(IB * (KC - 1), m * (KC - 1) + k - 1))
                ins = dve.scalar_tensor_tensor(out=u[:, :, k:S], in0=f[:, :, 0:S - k],
                                               scalar=conv_w[:, m, KC - 1 - k:KC - k], in1=u[:, :, k:S],
                                               op0=ALU.mult, op1=ALU.add)
                ins.then_inc(tap_done, 1)

            def silu_u(fi, m):
                dve.wait_ge(thu_ready, fi.count(IB, m + 1))
                u = u_buf[:, fi.parity, m, :]
                dve.scalar_tensor_tensor(out=u, in0=exp_t[:, m, :], scalar=1.0, in1=u, op0=ALU.add, op1=ALU.mult
                                         ).then_inc(u_ready, 1)

            def silu_z(fi, m):
                dve.wait_ge(thz_ready, fi.count(IB, m + 1))
                z = z_buf[:, fi.parity, m, :]
                dve.scalar_tensor_tensor(out=z, in0=z, scalar=1.0, in1=PROD_BANKS[IB + m][:, :], op0=ALU.add, op1=ALU.mult
                                         ).then_inc(z_ready, 1)

            def rest(fi):
                dve.wait_ge(hi_ready, fi.count(2, 2))
                dve.scalar_tensor_tensor(out=bc_rest[64:96, :], in0=PROD_BANKS[XP][64:96, :], scalar=half[64:96, 0:1],
                                         in1=bc3[64:96, fi.parity, :], op0=ALU.mult, op1=ALU.subtract
                                         ).then_inc(rest_ready, 1)

            def lowest(fi):
                dve.wait_ge(mid_ready, fi.count(1, 1))
                dve.tensor_tensor(bc3[0:32, fi.parity, :], bc_rest[64:96, :], bc_mid[64:96, :], ALU.subtract
                                  ).then_inc(parts_ready, 1)

            def one_less(fi, m):
                dve.wait_ge(exp_ready, fi.count(1, 1))
                dve.tensor_scalar(dtu[:, fi.parity, m, :], exp_t[:, m, :], 1.0, -1.0, ALU.add, ALU.add
                                  ).then_inc(w1_ready, 1)

            def drive(g, j):
                i = j // PAIRS
                dve.wait_ge(b_full, g.count(SLOTS, j + 1))
                if j % PAIRS == 0:
                    dve.wait_ge(dtu_ready, g.count(IB, i + 1))
                b = b_bank[:, j % 2, :, :]
                dve.tensor_tensor(b, dtu[:, g.parity, i, :].unsqueeze(1).to_broadcast([128, 2, CH]), b, ALU.mult
                                  ).then_inc(drive_ready, 1)

            def scan(g, j):
                dve.wait_ge(drive_ready, g.count(SLOTS, j + 1))
                dve.wait_ge(decay_full, g.count(2 * SLOTS, 2 * j + 2))
                need(dve, cm_done, g.count(SLOTS, j - 2))
                dve.tensor_tensor_scan(state[:, j % 3, :, :].rearrange("p a t -> p (a t)"),
                                       decay[:, j % 3, :, :, :].rearrange("p a b t -> p (a b t)"),
                                       b_bank[:, j % 2, :, :].rearrange("p a t -> p (a t)"),
                                       0.0, ALU.mult, ALU.add).then_inc(scan_done, 1)

            def gate_d(g, i):
                dve.wait_ge(k_full, g.count(KUSES, i + 1))
                if i == 0:
                    dve.wait_ge(wb_in, g.layers(16))
                dve.scalar_tensor_tensor(out=gated[:, i, :], in0=u_buf[:, g.parity, i, :], scalar=d_v[:, i:i + 1],
                                         in1=BACK_BANKS[i][:, :], op0=ALU.mult, op1=ALU.add).then_inc(g_ready, 1)

            def residual(g, k):
                dve.wait_ge(k_full, g.count(KUSES, IB + 1 + k))
                x = x_all[:, k, g.tokens()]
                dve.scalar_tensor_tensor(out=x, in0=BACK_BANKS[IB + k][0:KP, :], scalar=0.25, in1=x,
                                         op0=ALU.mult, op1=ALU.add).then_inc(x_ready, 1)

            def step(g, first=False, front=True, norm=True):
                f = g.plus(1)
                for j in range(SLOTS):
                    drive(g, j)
                    if front:
                        if j == 3:
                            tap(f, 0, 1)
                        if j in (4, 5, 6, 7, 8, 9):
                            tap(f, (j - 2) // 3, 1 + (j - 2) % 3)
                        if j == 12:
                            silu_u(f, 2)
                        if j == 13:
                            silu_z(f, 1)
                        if j == 14:
                            silu_z(f, 2)
                        if j == 15:
                            rest(f)
                        if j == 16:
                            lowest(f)
                        if j == 19:
                            one_less(f, 0)
                        if j == 21:
                            one_less(f, 2)
                    if j == 20:
                        gate_d(g, 1)
                    if j == 10 and not first:
                        residual(g.plus(-1), 0)
                    scan(g, j)
                    if j == 12:
                        gate_d(g, 0)
                    if front:
                        if j == 3:
                            tap(f, 0, 2)
                        if j == 10:
                            tap(f, 2, 3)
                        if j == 7:
                            silu_u(f, 0)
                        if j == 8:
                            silu_u(f, 1)
                        if j == 9:
                            silu_z(f, 0)
                        if j == 19:
                            one_less(f, 1)
                    if not first:
                        if j == 5:
                            gate_d(g.plus(-1), 2)
                        if j == 11:
                            residual(g.plus(-1), 1)

            p = Step(0, 0)
            for m in range(IB):
                for k in range(1, KC):
                    tap(p, m, k)
                silu_u(p, m)
            for m in range(IB):
                silu_z(p, m)
            rest(p)
            lowest(p)
            for m in range(IB):
                one_less(p, m)
            steps_loop(dve, step)
            last = Step(0, steps - 1)
            gate_d(last, 2)
            residual(last, 0)
            residual(last, 1)

            dve.wait_ge(x_ready, steps * KT)
            made = [0]

            def make(ins):
                made[0] += 1
                ins.then_inc(mchain, 1)

            make(dve.tensor_reduce(id_sum, ident[0:96, 0:96].rearrange("p (a e) -> p e a", a=3), AX.X, ALU.add))
            make(dve.memset(top4, LOW))
            make(dve.memset(g1o[GH:GH + 1, :], 1.0))
            make(dve.memset(selz, 0.0))
            make(dve.memset(small[:, 177:179], 0.0))
            make(dve.tensor_reduce(mid_w, nident[:, RR:3 * RR], AX.X, ALU.add))
            make(dve.tensor_reduce(mid_w2, nident[:, 5 * RR:6 * RR], AX.X, ALU.add))
            make(dve.tensor_reduce(low_w, nident[:, 2 * RR:3 * RR], AX.X, ALU.add))
            dve.wait_ge(mchain, made[0])
            make(dve.tensor_tensor(mid_w, mid_w, mid_w2, ALU.add))
            make(dve.memset(mid_z[64:128, :], -1.0))
            make(dve.memset(low_z[96:128, :], -1.0))
            for first in (0, 4):
                make(dve.tensor_copy(selz[:, :, first:first + 3, :],
                                     ident[:, :].rearrange("p (s r) -> p s r", s=SP).unsqueeze(2)
                                     .to_broadcast([128, SP, 3, RR])))
            make(dve.tensor_copy(gsel.rearrange("p b (m h) -> p (b m) h", h=HD),
                                 id_sum.unsqueeze(2).to_broadcast([96, 32, HD])))
            dve.wait_ge(mchain, made[0])
            dve.sem_inc(mix_open, 1)
            MC = made[0]
            ML = 5 + TILES * 7

            for s in range(SP):
                dve.wait_ge(w1_hi_ready, s + 1)
                if s > 0:
                    dve.wait_ge(w1_built, s)
                dve.scalar_tensor_tensor(out=w1_rest, in0=w1_hi, scalar=mid_w, in1=b_all, op0=ALU.mult, op1=ALU.add
                                         ).then_inc(w1_rest_ready, 1)
                dve.wait_ge(w1_mid_ready, s + 1)
                dve.scalar_tensor_tensor(out=w1_s[:, s, :], in0=w1_mid, scalar=low_w, in1=w1_rest,
                                         op0=ALU.mult, op1=ALU.add).then_inc(w1_built, 1)

            def z_less_high(c, s):
                dve.wait_ge(zhi_ready, c * SP + (s + 1))
                if s > 0:
                    dve.wait_ge(z_built, c * SP + s)
                dve.scalar_tensor_tensor(out=z_rest, in0=z_hi, scalar=mid_z, in1=zs_bank(s), op0=ALU.mult, op1=ALU.add
                                         ).then_inc(zrest_ready, 1)

            def z_less_middle(c, s):
                dve.wait_ge(zmid_ready, c * SP + (s + 1))
                if s > 1:
                    dve.wait_ge(h1_full, c * (SP * NBLK) + (s - 1) * NBLK)
                dve.scalar_tensor_tensor(out=z_s[:, s % 2, :], in0=z_mid, scalar=low_z, in1=z_rest,
                                         op0=ALU.mult, op1=ALU.add).then_inc(z_built, 1)

            def bc(v):
                return v.unsqueeze(2).to_broadcast([128, TILES, H])

            def apart():
                dve.memset(small[:, 176:177], 0.0)

            dve.wait_ge(mw_in, 16 * W_LOADS)
            with dve.Fori(0, NCH) as c:
                at = [0]

                def mlink(ins):
                    at[0] += 1
                    ins.then_inc(mchain, 1)
                    dve.wait_ge(mchain, c * ML + (MC + at[0]))

                dve.wait_ge(xsq_ready, c + 1)
                dve.tensor_reduce(sm_ss, sqm, AX.X, ALU.add).then_inc(xss_ready, 1)
                dve.wait_ge(xrs_ready, c + 1)
                mlink(dve.tensor_tensor(h2.rearrange("p (a b) h -> p a b h", a=2), xt_p,
                                        sm_rs.rearrange("p (a b) -> p a b", a=2).unsqueeze(3).to_broadcast([128, 2, 2, H]),
                                        ALU.mult))
                mlink(dve.tensor_tensor(h2, h2, fw_v.unsqueeze(1).to_broadcast([128, TILES, H]), ALU.mult))
                dve.wait_ge(h_back, c * 16 + 16)
                mlink(dve.tensor_tensor(h2, h2, h_in, ALU.add))
                mlink(dve.tensor_reduce(sm_sum, h2, AX.X, ALU.add))
                mlink(dve.tensor_scalar(sm_mean, sm_sum, 1.0 / H, None, ALU.mult))
                dve.tensor_tensor(xf, h2, bc(sm_mean), ALU.subtract).then_inc(hc_ready, 1)
                dve.wait_ge(hsq_ready, c + 1)
                dve.tensor_reduce(sm_var, sqm, AX.X, ALU.add).then_inc(hvar_ready, 1)
                dve.wait_ge(hrs_ready, c + 1)
                dve.tensor_tensor(xf, xf, bc(sm_rstd), ALU.mult).then_inc(xf_ready, 1)
                z_less_high(c, 0)
                z_less_middle(c, 0)
                for t in range(TILES):
                    p = sc_p[t % 2][:, :]
                    p3 = p.rearrange("p (s m) -> p s m", s=SP)
                    dve.wait_ge(sc_full, c * TILES + (t + 1))
                    apart()
                    for s in range(SP):
                        ins = dve.max(top8[:, s, :], p3[:, s, :])
                    mlink(ins)
                    mlink(dve.tensor_copy(top4[:, :, 0:TOPK], top8[:, :, 0:TOPK]))
                    apart()
                    for s in range(SP):
                        ins = dve.match_replace(rep[:, s * ME:(s + 1) * ME], top4[:, s, :], p3[:, s, :], LOW)
                    dve.tensor_tensor(dif.rearrange("p (s m) -> p s m", s=SP), p3,
                                      top8[:, :, 0:1].to_broadcast([128, SP, ME]), ALU.subtract).then_inc(dif_ready, 1)
                    mlink(ins)
                    mlink(dve.tensor_tensor(rep, p, rep, ALU.not_equal))
                    dve.wait_ge(exs_ready, c * TILES + (t + 1))
                    mlink(dve.tensor_tensor(exs, exs, rep, ALU.mult))
                    mlink(dve.tensor_reduce(den, exs.rearrange("p (s m) -> p s m", s=SP), AX.X, ALU.add))
                    mlink(dve.reciprocal(rden, den))
                    dve.tensor_tensor(wt.rearrange("p (s m) -> p s m", s=SP), exs.rearrange("p (s m) -> p s m", s=SP),
                                      rden.unsqueeze(2).to_broadcast([128, SP, ME]), ALU.mult).then_inc(wt_ready, 1)
                dve.wait_ge(whi_ready, c + 1)
                dve.tensor_tensor(wrest, wt32, w_parts[0], ALU.subtract).then_inc(wrest_ready, 1)
                dve.wait_ge(wmid_ready, c + 1)
                dve.tensor_tensor(w_parts[2], wrest, w_parts[1], ALU.subtract).then_inc(wlo_ready, 1)
                for b in range(SP * NBLK):
                    dve.wait_ge(gelu_done, c * (SP * NBLK) + (b + 1))
                    dve.wait_ge(gate_full, c * (SP * NBLK) + (b + 1))
                    if b >= 3:
                        dve.wait_ge(hg_used, c * (SP * NBLK) + (b - 2))
                    dve.tensor_tensor(hid[:, 3 + b % 3, :], hid[:, b % 3, :], gate_p[:, b % 2, :], ALU.mult
                                      ).then_inc(hg_ready, 1)
                    if b % NBLK == 5 and b // NBLK + 1 < SP:
                        z_less_high(c, b // NBLK + 1)
                    if b % NBLK == 8 and b // NBLK + 1 < SP:
                        z_less_middle(c, b // NBLK + 1)
                dve.wait_ge(o_full, c + 1)
                dve.tensor_tensor(xf.rearrange("p (a b) h -> p a b h", a=2), xt_p,
                                  h2.rearrange("p (a b) h -> p a b h", a=2), ALU.add).then_inc(o_ready, 1)
                dve.wait_ge(o_ready, c + 1)
                dve.sem_inc(mix_open, 1)
                assert at[0] == ML

        @block.tensor
        def _(pe):
            pe.wait_ge(consts, 9)
            for g in range(GR):
                pe.wait_ge(x0_ready, g + 1)
                for t in range(GB // CB):
                    for k in range(KT):
                        need(pe, x0_kept, (g * (GB // CB) + t) * KT + k - 1)
                        for b in range(CB):
                            ins = pe.transpose((f_bank, k_bank)[k][0:KP, b * S:(b + 1) * S],
                                               x0_g[g % 2][:, t * CB + b, k * KP:(k + 1) * KP], ident[:, :])
                        ins.then_inc(x0_turned, 1)

            def start_product(fi, use, first=False):
                b = fi.plus(-2)
                if use == 0:
                    if first:
                        pe.wait_ge(ln_ready, 1)
                    else:
                        pe.wait_ge(ndt_ready, fi.count(IB, -2))
                elif use == 1 and not first:
                    pe.wait_ge(ndt_ready, fi.count(IB, -1))
                elif use in (2, 3, 4):
                    pe.wait_ge(tap_done, fi.count(IB * (KC - 1), (use - 1) * (KC - 1)))
                elif use == 5 and not first:
                    pe.wait_ge(ndt_ready, fi.count(IB, 0))
                    need(pe, x_ready, b.count(KT, KT))
                elif use == XP:
                    if first:
                        pe.wait_ge(z_ready, 1)
                    else:
                        pe.wait_ge(g_ready, fi.count(IB, 1 - IB))
                elif use in (DT, DT + 1):
                    pe.wait_ge(z_ready, fi.count(IB, use - DT + 2))
                elif use == DT + 2:
                    pe.wait_ge(rest_ready, fi.count(1, 1))
                elif use == SOFT:
                    pe.wait_ge(rel_ready, fi.count(IB, 1))
                elif use == SOFT + 1:
                    if first:
                        pe.wait_ge(rel_ready, IB)
                    else:
                        pe.wait_ge(g_ready, fi.count(IB, 2 - IB))
                elif use == SOFT + 2:
                    if first:
                        pe.wait_ge(c_kept, NST)
                    else:
                        pe.wait_ge(g_ready, fi.count(IB, 0))
                return PROD_BANKS[use]

            def norm_sum(fi, first=False):
                pe.wait_ge(sq_ready, fi.count(1, 1))
                if first:
                    pe.wait_ge(x0_kept, 2 * NCH)
                else:
                    pe.wait_ge(rel_ready, fi.plus(-1).count(IB, 1))
                for k in range(KT):
                    ins = pe.matmul(f_bank[0:KP, :], onesm[:, :], xn[:, k, :], start=(k == 0), stop=(k == KT - 1))
                ins.then_inc(norm_full, 1)

            def in_proj(fi, m, first=False):
                if m == 0:
                    pe.wait_ge(xn_ready, fi.count(1, 1))
                bank = start_product(fi, m, first)
                for k in range(KT):
                    ins = pe.matmul(bank[:, :], w_in_v[:, k, m * 128:(m + 1) * 128], xn[:, k, :],
                                    start=(k == 0), stop=(k == KT - 1))
                ins.then_inc(f_full, 1)

            def x_proj(fi, first=False):
                pe.wait_ge(u_ready, fi.count(IB, IB))
                bank = start_product(fi, XP, first)
                for k in range(IB):
                    ins = pe.matmul(bank[0:96, :], w_x_v[:, k, :], u_buf[:, fi.parity, k, :],
                                    start=(k == 0), stop=(k == IB - 1))
                ins.then_inc(f_full, 1)

            def dt_proj(fi, m):
                if m == 0:
                    pe.wait_ge(hi_ready, fi.count(2, 1))
                bank = start_product(fi, DT + m)
                pe.matmul(bank[:, :], wdt[:, m * 128:(m + 1) * 128], dtr[:, :], start=True, stop=True
                          ).then_inc(f_full, 1)

            def softplus_first(fi, m, ln_read, first=False):
                if m == 0:
                    pe.wait_ge(exp_ready, fi.count(1, 1))
                    if ln_read:
                        pe.wait_ge(ln_ready, fi.count(1, 2))
                bank = start_product(fi, SOFT + m, first)
                pe.matmul(bank[:, :], ident[:, :], exp_t[:, m, :], start=True, stop=False)
                pe.matmul(bank[:, :], ident[:, :], rel_t[:, m, :], start=False, stop=False)

            def softplus_second(fi, m):
                if m == 0:
                    pe.wait_ge(ln1_ready, fi.count(1, 1))
                pe.wait_ge(w1_ready, fi.count(IB, m + 1))
                bank = PROD_BANKS[SOFT + m]
                pe.matmul(bank[:, :], ident[:, :], ndt[:, fi.parity, m, :], start=False, stop=False)
                pe.matmul(bank[:, :], nident[:, :], dtu[:, fi.parity, m, :], start=False, stop=True
                          ).then_inc(soft_full, 1)

            def spread_b(g, j):
                if j == 0:
                    pe.wait_ge(parts_ready, g.count(2, 2))
                    pe.wait_ge(hi_ready, g.count(2, 2))
                need(pe, scan_done, g.count(SLOTS, j - 1))
                for k in range(2):
                    n = 2 * (j % PAIRS) + k
                    ins = pe.matmul(b_bank[:, j % 2, k, :], sel[:, n, :], bc3[:, g.parity, :], start=True, stop=True)
                ins.then_inc(b_full, 1)

            def spread_c(g, n):
                if n == 0:
                    pe.wait_ge(parts_ready, g.count(2, 2))
                    pe.wait_ge(hi_ready, g.count(2, 2))
                    pe.wait_ge(rel_ready, g.count(IB, 2))
                need(pe, c_kept, g.count(NST, n))
                pe.matmul(c_bank[:, :], sel[:, NST + n, :], bc3[:, g.parity, :], start=True, stop=True
                          ).then_inc(c_full, 1)

            def sum_states(g, j):
                i, q = divmod(j, PAIRS)
                if q == 0:
                    need(pe, y_kept, g.count(IB, i))
                pe.wait_ge(cm_done, g.count(SLOTS, j + 1))
                for k in range(2):
                    for t in range(TILES):
                        ins = pe.matmul(y_bank[:, t * 128:(t + 1) * 128], state_c[:, j % 3, k, t * 128:(t + 1) * 128],
                                        ident[:, :], start=(q == 0 and k == 0 and t == 0),
                                        stop=(q == PAIRS - 1 and k == 1), is_transpose=True, skip_group_check=True)
                ins.then_inc(turned, 1)

            def y_back(g, i, front=True, final=False):
                pe.wait_ge(y_kept, g.count(IB, i + 1))
                if i == 2:
                    pe.wait_ge(c_kept, g.count(NST, NST) if final else g.plus(1).count(NST, NST))
                elif front:
                    if i == 0:
                        pe.wait_ge(z_ready, g.plus(1).count(IB, 1))
                    else:
                        pe.wait_ge(rel_ready, g.plus(1).count(IB, IB))
                elif i == 1:
                    pe.wait_ge(g_ready, g.count(IB, 1))
                else:
                    pe.wait_ge(ndt_ready, g.count(IB, 2))
                for t in range(TILES):
                    ins = pe.transpose(BACK_BANKS[i][:, t * 128:(t + 1) * 128], y_rows[:, t * 128:(t + 1) * 128],
                                       ident[:, :])
                ins.then_inc(k_full, 1)

            def out_proj(g, m, final=False):
                pe.wait_ge(gz_ready, g.count(IB, IB))
                if m == 0 and not final:
                    pe.wait_ge(ndt_ready, g.plus(1).count(IB, IB))
                if m == 1:
                    pe.wait_ge(x_ready, g.count(KT, 1))
                for k in range(IB):
                    ins = pe.matmul(BACK_BANKS[IB + m][0:KP, :], w_out_v[:, k, m * KP:(m + 1) * KP], gated[:, k, :],
                                    start=(k == 0), stop=(k == IB - 1))
                ins.then_inc(k_full, 1)

            def step(g, first=False, front=True, norm=True):
                f, h = g.plus(1), g.plus(2)
                b = g.plus(-1)
                for j in range(SLOTS):
                    if j + 1 < SLOTS:
                        spread_b(g, j + 1)
                    elif front:
                        spread_b(f, 0)
                    if j <= PAIRS - C_EARLY:
                        spread_c(g, 2 * (j + C_EARLY - 1) + 1)
                    if j > C_SLOT and front:
                        spread_c(f, 2 * (j - C_SLOT - 1) + 1)
                    if j >= 3:
                        sum_states(g, j - 3)
                    elif not first:
                        sum_states(b, SLOTS + j - 3)
                    if j < PAIRS - C_EARLY:
                        spread_c(g, 2 * (j + C_EARLY))
                    if j >= C_SLOT and front:
                        spread_c(f, 2 * (j - C_SLOT))
                    if j == 4 and not first:
                        y_back(b, 2)
                    if j in (11, 19):
                        y_back(g, (j - 11) // 8, front)
                    if j == 6:
                        softplus_first(g, 2, False, first)
                    if j == 7:
                        softplus_second(g, 2)
                    if j in (9, 10) and not first:
                        out_proj(b, j - 9)
                    if front:
                        if j in (0, 2, 5, 8, 11, 12):
                            in_proj(f, (0, 2, 5, 8, 11, 12).index(j))
                        if j == 13:
                            x_proj(f)
                        if j == 15:
                            dt_proj(f, 0)
                            dt_proj(f, 1)
                        if j == 16:
                            dt_proj(f, 2)
                    if norm and j == 17:
                        norm_sum(h)
                    if front:
                        if j in (19, 21):
                            softplus_first(f, (j - 19) // 2, norm)
                        if j in (20, 22):
                            softplus_second(f, (j - 20) // 2)

            p = Step(0, 0)
            norm_sum(p, True)
            for m in range(2 * IB):
                in_proj(p, m, True)
            x_proj(p, True)
            for m in range(IB):
                dt_proj(p, m)
            norm_sum(p.plus(1))
            for m in range(2):
                softplus_first(p, m, True, True)
                softplus_second(p, m)
            for n in range(2 * C_EARLY - 1):
                spread_c(p, n)
            spread_b(p, 0)
            steps_loop(pe, step)
            last = Step(0, steps - 1)
            for j in range(SLOTS - 3, SLOTS):
                sum_states(last, j)
            y_back(last, 2, final=True)
            out_proj(last, 0, final=True)
            out_proj(last, 1)

            pe.wait_ge(mw_in, 16 * W_LOADS)
            for s in range(SP):
                if s > 0:
                    pe.wait_ge(w1_rest_ready, s)
                for i in range(NW1 // CH):
                    ins = pe.matmul(b_bank[:, i // 2, i % 2, :], selz_of(s), w1_c[:, i * CH:(i + 1) * CH],
                                    start=True, stop=True)
                ins.then_inc(w1_full, 1)
            pe.wait_ge(w1_built, SP)

            def z_to_groups(c, s):
                if s > 1:
                    pe.wait_ge(zrest_ready, c * SP + s)
                pe.matmul(zs_bank(s), selz_of(s), z_t, start=True, stop=True).then_inc(zs_full, 1)

            with pe.Fori(0, NCH) as c:
                pe.wait_ge(mix_open, c + 1)
                pe.wait_ge(xs_ready, c + 1)
                for t in range(TILES):
                    for k in range(KT):
                        ins = pe.transpose(xt_p[:, t // 2, t % 2, k * KP:(k + 1) * KP], xs[:, k, t * 128:(t + 1) * 128],
                                           ident[0:KP, 0:KP])
                ins.then_inc(xt_full, 1)
                pe.wait_ge(xf_ready, c + 1)
                for k in range(KT):
                    for t in range(TILES):
                        ins = pe.transpose(xft_p[:, k, t * 128:(t + 1) * 128], xf[:, t, k * KP:(k + 1) * KP], ident[:, :])
                ins.then_inc(xft_full, 1)
                pe.wait_ge(xft_ready, c + 1)
                for k in range(KT):
                    ins = pe.matmul(y_bank[:, :], p_v[:, k, :], xf_t[:, k, :], start=(k == 0), stop=(k == KT - 1))
                ins.then_inc(zt_full, 1)
                pe.wait_ge(zt_ready, c + 1)
                z_to_groups(c, 0)
                for t in range(TILES + 1):
                    if t < TILES:
                        if t >= 2:
                            pe.wait_ge(wt_ready, c * TILES + (t - 1))
                        pe.matmul(sc_p[t % 2][:, :], z_t[:, t * 128:(t + 1) * 128], cb_v, start=True, stop=True
                                  ).then_inc(sc_full, 1)
                    if t >= 1:
                        pe.wait_ge(wt_ready, c * TILES + t)
                        if t >= 2:
                            pe.wait_ge(wt_kept, c * TILES + (t - 1))
                        for sp in range(4):
                            ins = pe.transpose(c_bank[:, sp * 128:(sp + 1) * 128], wt[:, sp * 128:(sp + 1) * 128],
                                               ident[:, :])
                        ins.then_inc(wt_full, 1)
                pe.wait_ge(wt_kept, c * TILES + TILES)
                pe.wait_ge(wlo_ready, c + 1)
                for b in range(SP * NBLK + 2):
                    if b < SP * NBLK:
                        s, blk = divmod(b, NBLK)
                        if blk == 0:
                            pe.wait_ge(z_built, c * SP + (s + 1))
                        if b >= 2:
                            pe.wait_ge(gelu_done, c * (SP * NBLK) + (b - 1))
                        pe.matmul(h1_p[:, b % 2, :], w1_s[:, s, blk * 128:(blk + 1) * 128], z_s[:, s % 2, :],
                                  start=True, stop=True).then_inc(h1_full, 1)
                        if b % (2 * NBLK) == 0:
                            pe.wait_ge(g_in[(s // 2) % 2], c * (2 * 192) + (s // 4 + 1) * 192)
                        if b >= 2:
                            pe.wait_ge(hg_ready, c * (SP * NBLK) + (b - 1))
                        q = 2 * (s % 2) + blk // 8
                        ins = pe.matmul(gate_p[:, b % 2, :], gsel[:, blk % 8, :], g_parts[:, (s // 2) % 2, q, :],
                                        start=True, stop=True)
                        ins.then_inc(gate_full, 1)
                        if blk == 2 and s + 1 < SP:
                            z_to_groups(c, s + 1)
                    if b >= 2:
                        d = b - 2
                        s, blk = divmod(d, NBLK)
                        sp, r = s // 2, 32 * (s // 2)
                        pe.wait_ge(hg_ready, c * (SP * NBLK) + (d + 1))
                        if d % (2 * NBLK) == 0:
                            pe.matmul(y_bank[r:r + 32, :], b2_v[:, sp, :], wt32[:, sp, :], start=True, stop=False)
                        last = d % (2 * NBLK) == 2 * NBLK - 1
                        ins = pe.matmul(y_bank[r:r + 32, :], w2_v[d // 64][:, d % 64, :], hid[:, 3 + d % 3, :], start=False, stop=last)
                        ins.then_inc(hg_used, 1)
                pe.wait_ge(comb_ready, c + 1)
                pe.matmul(f_bank[0:GH, :], g1_v, comb, start=True, stop=True).then_inc(g1_full, 1)
                pe.wait_ge(g1_ready, c + 1)
                for t in range(TILES):
                    ins = pe.matmul(xt_p[:, t // 2, t % 2, :], g1o[0:GH + 1, t * 128:(t + 1) * 128], g2_v,
                                    start=(t % 2 == 0), stop=True, skip_group_check=True)
                ins.then_inc(o_full, 1)


_INS = ['ids', 'type_ids', 'tok_w', 'pos_w', 'type_w', 'gamma', 'beta', 'w_in', 'w_front', 'w_dt', 'w_back', 'a_log',
        'final_w', 'p_w', 'c_blocks', 'w1', 'b1', 'w2', 'b2', 'g1', 'g1b', 'g2', 'g2b']


def lay_out(inputs):
    import numpy as np

    a = {k: np.asarray(v) for k, v in inputs.items()}
    m = {k[8:]: v for k, v in a.items() if k.startswith("L0_attn_")}
    f = {k[7:]: v for k, v in a.items() if k.startswith("L0_ffn_")}
    cat = np.concatenate

    def blocks(v):
        v = v.reshape(NL, IB, 128, -1)
        return v.transpose(0, 2, 1, 3).reshape(NL, 128, -1)

    x_proj = np.zeros((NL, 96, IN), np.float32)
    x_proj[:, :R] = m["x_proj_w"][:, :R]
    x_proj[:, 64:] = m["x_proj_w"][:, R:]
    in_t = m["in_proj_w"].transpose(0, 2, 1).reshape(NL, KT, KP, 2 * IN).transpose(0, 2, 1, 3).reshape(NL, KP, -1)
    w_in = cat([in_t, m["norm_w"].reshape(NL, KT, KP).transpose(0, 2, 1)], 2)
    w_front = cat([blocks(x_proj.transpose(0, 2, 1)), blocks(m["conv_w"]), blocks(m["conv_b"]),
                   blocks(m["dt_proj_b"])], 2)
    w_back = cat([blocks(m["out_proj_w"].transpose(0, 2, 1)), blocks(m["D"])], 2)
    c_blocks = np.zeros((SP, RR, SP, ME), np.float32)
    w2 = np.zeros((SP, NBLK, EB, HD, 2, RR), np.float32)
    b2 = np.zeros((SP // 2, 2, ME, 2, RR), np.float32)
    for s in range(SP):
        c_blocks[s, :, s] = f["C"][s].T
        w2[s, :, :, :, s % 2] = f["W2"][s].reshape(NBLK, EB, HD, RR)
        b2[s // 2, s % 2, :, s % 2] = f["b2"][s]
    return {
        "ids": a["x"].T, "type_ids": a["mask_BS_i1_0"].T,
        "tok_w": a["L0_tok_tok_w"], "pos_w": a["L0_tok_pos_w"], "type_w": a["L0_tok_type_w"],
        "gamma": a["L0_tok_gamma"], "beta": a["L0_tok_beta"],
        "w_in": w_in, "w_front": w_front, "w_dt": m["dt_proj_w"].transpose(0, 2, 1), "w_back": w_back,
        "a_log": blocks(m["A_log"]), "final_w": m["final_norm_w"],
        "p_w": f["P"].transpose(1, 0, 2).reshape(KT, KP, SP * RR).transpose(1, 0, 2),
        "c_blocks": c_blocks.reshape(SP * RR, SP * ME),
        "w1": f["W1"].transpose(0, 2, 1, 3).reshape(SP * RR, ME * HD),
        "b1": f["b1"].reshape(SP * NBLK, EB * HD).T,
        "w2": w2.reshape(SP * NBLK, EB * HD, 2 * RR).transpose(1, 0, 2),
        "b2": b2.reshape(SP // 2, 2 * ME, 2 * RR).transpose(1, 0, 2),
        "g1": f["G1"], "g1b": f["g1b"].reshape(GH, 1),
        "g2": f["G2"], "g2b": f["g2b"],
    }


def kernel(**inputs):
    import numpy as np
    import concourse.bacc as bacc
    from concourse.bass_utils import run_bass_kernel_spmd

    nc = bacc.Bacc("TRN2", target_bir_lowering=False, num_devices=1)
    laid = lay_out(inputs)
    arrays, args = {}, []
    for name in _INS:
        v = np.ascontiguousarray(laid[name])
        arrays[f"in_{name}_dram"] = v
        args.append(nc.dram_tensor(f"in_{name}_dram", v.shape, mybir.dt.from_np(v.dtype), kind="ExternalInput").ap())
    h_scratch = nc.dram_tensor("h_scratch", (S, NB, H), F32, kind="Internal").ap()
    out = nc.dram_tensor("out_dram", (NB, S, H), F32, kind="ExternalOutput").ap()
    lm_tower(nc, *args, h_scratch, out)
    r = run_bass_kernel_spmd(nc, [arrays], core_ids=[0])
    return r.results[0]["out_dram"]
```
